# Optimizing a Trainium2 kernel written in Bass

```python
import numpy as np
import jax
import jax.numpy as jnp

def _softmax(x, axis=-1):
    return jax.nn.softmax(x, axis=axis)

def _gelu(x):
    return jax.nn.gelu(x, approximate=True)

def _silu(x):
    return jax.nn.silu(x)

def _sigmoid(x):
    return jax.nn.sigmoid(x)

def _layernorm(x, axis=-1, eps=1e-05):
    m = jnp.mean(x, axis=axis, keepdims=True)
    v = jnp.var(x, axis=axis, keepdims=True)
    return (x - m) / jnp.sqrt(v + eps)

def _scatter_add(tgt, idx, src, axis=0):
    return tgt.at[idx].add(src)

def _segment_sum(src, seg, n):
    return jax.ops.segment_sum(src, seg, n)
kernel_name = 'mk_cond_resid_d2_seqx_r4_99b236'

def setup_inputs(seed: int=0):
    np.random.seed(seed)
    _w = jnp.asarray

    def _rec_inputs():
        import jax
        import jax.numpy as jnp
        _rk = jax.random.key(seed)
        x = 7.22e-05 + 1 * jax.random.normal(jax.random.fold_in(_rk, 1), (32, 64, 1024), jnp.float32)
        _lenS = 64 - jax.random.randint(jax.random.fold_in(_rk, 7), (32,), 0, max(1, 64 // 4) + 1, jnp.int32)
        _lenS2 = 64 - jax.random.randint(jax.random.fold_in(_rk, 8), (32,), 0, max(1, 64 // 4) + 1, jnp.int32)
        itok_B_2_6 = jax.random.randint(jax.random.fold_in(_rk, 11), (32,), 2, 7, jnp.int32)
        condB_codebook = -0.0625 + 0.715345 * jax.random.normal(jax.random.fold_in(_rk, 12), (32,), jnp.float32)
        return (x, itok_B_2_6, condB_codebook)
    x, itok_B_2_6, condB_codebook = _rec_inputs()

    def _L0_cond_setup():
        import jax, jax.numpy as jnp
        import numpy as np
        B, N, H, F = (4, 128, 1024, 2752)
        L, R, RANK = (1, 16, 16)
        SCALE = 0.5
        key = jax.random.key(seed)
        ks = jax.random.split(key, 12)
        nrm = lambda k, shape, fan: jax.random.normal(k, shape, jnp.float32) * fan ** (-0.5)
        inp = {'x': jax.random.normal(ks[0], (B, N, H), jnp.float32), 'W_gate': nrm(ks[1], (F, H), H), 'W_up': nrm(ks[2], (F, H), H), 'W_down': nrm(ks[3], (H, F), F), 'A_gate': nrm(ks[4], (L, R, RANK, H), H), 'B_gate': nrm(ks[5], (L, R, F, RANK), RANK), 'A_up': nrm(ks[6], (L, R, RANK, H), H), 'B_up': nrm(ks[7], (L, R, F, RANK), RANK), 'A_down': nrm(ks[8], (L, R, RANK, F), F), 'B_down': nrm(ks[9], (L, R, H, RANK), RANK), 'lora_indices': jax.random.randint(ks[10], (B,), 0, R), 'layer_idx': 0}
        return inp
    _L0_cond_all = _L0_cond_setup()
    _L0_cond_in = {k: v for k, v in _L0_cond_all.items() if k in ('W_gate', 'W_up', 'W_down', 'A_gate', 'B_gate', 'A_up', 'B_up', 'A_down', 'B_down')}
    del _L0_cond_all

    def _L1_cond_setup():
        import jax, jax.numpy as jnp
        import numpy as np
        GROUP = 128
        LORA_ALPHA = 32.0
        LORA_RANK = 64
        key = jax.random.key(seed)
        k1, k2, k3, k4 = jax.random.split(key, 4)
        O, I = (1024, 1024)
        x = jax.random.normal(k1, (4, 512, I), dtype=jnp.float32)
        weight = jax.random.normal(k2, (O, I), dtype=jnp.float32) * 0.02
        wg = weight.reshape(O, I // GROUP, GROUP)
        scale_log = jnp.log(jnp.clip(jnp.max(jnp.abs(wg), axis=2, keepdims=True), 1e-05))
        codebook = jnp.array([-1.0, -0.25, 0.0, 1.0], dtype=jnp.float32)
        lora_A = jax.random.normal(k3, (LORA_RANK, I), dtype=jnp.float32) * 0.02
        lora_B = jax.random.normal(k4, (O, LORA_RANK), dtype=jnp.float32) * 0.02
        return {'x': x, 'weight': weight, 'scale_log': scale_log, 'codebook': codebook, 'lora_A': lora_A, 'lora_B': lora_B}
    _L1_cond_all = _L1_cond_setup()
    _L1_cond_in = {k: v for k, v in _L1_cond_all.items() if k in ('weight', 'scale_log', 'lora_A', 'lora_B')}
    del _L1_cond_all
    return {'x': x, 'itok_B_2_6': itok_B_2_6, 'condB_codebook': condB_codebook, 'L0_cond_W_gate': _L0_cond_in['W_gate'], 'L0_cond_W_up': _L0_cond_in['W_up'], 'L0_cond_W_down': _L0_cond_in['W_down'], 'L0_cond_A_gate': _L0_cond_in['A_gate'], 'L0_cond_B_gate': _L0_cond_in['B_gate'], 'L0_cond_A_up': _L0_cond_in['A_up'], 'L0_cond_B_up': _L0_cond_in['B_up'], 'L0_cond_A_down': _L0_cond_in['A_down'], 'L0_cond_B_down': _L0_cond_in['B_down'], 'L1_cond_weight': _L1_cond_in['weight'], 'L1_cond_scale_log': _L1_cond_in['scale_log'], 'L1_cond_lora_A': _L1_cond_in['lora_A'], 'L1_cond_lora_B': _L1_cond_in['lora_B']}

def reference(x, itok_B_2_6, condB_codebook, L0_cond_W_gate, L0_cond_W_up, L0_cond_W_down, L0_cond_A_gate, L0_cond_B_gate, L0_cond_A_up, L0_cond_B_up, L0_cond_A_down, L0_cond_B_down, L1_cond_weight, L1_cond_scale_log, L1_cond_lora_A, L1_cond_lora_B):
    import jax
    import jax.numpy as jnp

    def _L0_cond_ref(x, W_gate, W_up, W_down, A_gate, B_gate, A_up, B_up, A_down, B_down, lora_indices, layer_idx):
        import jax, jax.numpy as jnp
        import numpy as np
        B, N, H, F = (4, 128, 1024, 2752)
        L, R, RANK = (1, 16, 16)
        SCALE = 0.5

        def lora_add(base, inp, A, B):
            Ab = A[layer_idx][lora_indices]
            Bb = B[layer_idx][lora_indices]
            t = jnp.einsum('bri,bni->bnr', Ab, inp)
            return base + jnp.einsum('bor,bnr->bno', Bb, t) * SCALE
        gate = lora_add(jnp.einsum('bnh,fh->bnf', x, W_gate), x, A_gate, B_gate)
        up = lora_add(jnp.einsum('bnh,fh->bnf', x, W_up), x, A_up, B_up)
        act = jax.nn.silu(gate) * up
        down = lora_add(jnp.einsum('bnf,hf->bnh', act, W_down), act, A_down, B_down)
        return down

    def _L1_cond_ref(x, weight, scale_log, codebook, lora_A, lora_B):
        import jax, jax.numpy as jnp
        import numpy as np
        GROUP = 128
        LORA_ALPHA = 32.0
        LORA_RANK = 64
        O, I = weight.shape
        lora_delta = lora_B @ lora_A * (LORA_ALPHA / LORA_RANK)
        cb = codebook / jnp.clip(jnp.max(jnp.abs(codebook)), 1e-08)
        scale = jnp.exp(scale_log)
        wg = (weight + lora_delta).reshape(O, I // GROUP, GROUP)
        normalized = wg / scale
        thresholds = (cb[:-1] + cb[1:]) * 0.5
        idx = jnp.searchsorted(thresholds, normalized, side='left')
        quantized = cb[idx]
        w = jax.lax.stop_gradient(quantized - normalized) + normalized
        w_q = (w * scale).reshape(O, I)
        w_eff = w_q + lora_delta
        return x @ w_eff.T
    x = x + _L0_cond_ref(x, L0_cond_W_gate, L0_cond_W_up, L0_cond_W_down, L0_cond_A_gate, L0_cond_B_gate, L0_cond_A_up, L0_cond_B_up, L0_cond_A_down, L0_cond_B_down, itok_B_2_6, 0)
    x = x + _L1_cond_ref(x, L1_cond_weight, L1_cond_scale_log, condB_codebook, L1_cond_lora_A, L1_cond_lora_B)
    return x

_drawn_inputs = setup_inputs


def setup_inputs(seed=0):
    import zlib

    import numpy as np

    out = dict(_drawn_inputs(seed))
    spreads = {}
    factors = {}
    for name, (base, spread) in spreads.items():
        noise = np.random.default_rng([zlib.crc32(name.encode()), seed]).standard_normal(out[name].shape)
        drawn = base * np.exp(spread * noise) if base else spread * noise
        out[name] = jnp.asarray(drawn.astype(out[name].dtype))
    for name, factor in factors.items():
        out[name] = (out[name] * factor).astype(out[name].dtype)
    return out
```

```python
import concourse.bass as bass
from concourse import mybir
from contextlib import ExitStack

F32 = mybir.dt.float32
F32R = mybir.dt.float32r
I32 = mybir.dt.int32
U8 = mybir.dt.uint8
ALU = mybir.AluOpType
ACT = mybir.ActivationFunctionType
AX = mybir.AxisListType

P = 128
BATCH, SEQ, H = 32, 64, 1024
F = 2752
RANK, NADAPT = 16, 16
LRANK = 64
NCODE = 32
TG = 512
NG = BATCH * SEQ // TG
BG = TG // SEQ
NPAIR = BG // 2
KT = H // P
NT = F // P
FREST = F - NT * P
FT = NT + 1
FC = 3
HT = H // P
UNIT = KT * P

U_A, U_P = 0, 2
U_M = U_P + 2 * NT
U_AD = U_M + 1
U_D = U_AD + FC
U_FFN = U_D + FC * HT
SLOTS = 4
LN_B = FT + HT

PIECES = [(256 * i, 256) for i in range(5)] + [(1280, 384), (1664, 384)]
QCOLS = sum(w for _, w in PIECES)
QW = max(w for _, w in PIECES)
NQ = len(PIECES) * NG
assert QCOLS * NG == KT * H and U_FFN % SLOTS == 0
NPIECE = len(PIECES)
BUFFERS = 2
QSTEPS = 4 + 2 * (NCODE - 1) + 4

HALF = float(0.5)
LOG2E = 1.4426950408889634
LN2_HI, LN2_LO = 0.693359375, -2.12194440e-4
EXP_POLY = [1.9875691500e-4, 1.3981999507e-3, 8.3334519073e-3, 4.1665795894e-2, 1.6666665459e-1,
            5.0000001201e-1]
ROUND = 12582912.0


def build(nc, x_in, idx_in, code_in, w_in, agu_in, bgu_in, ad_in, bd_in, qw_in, slog_in, qa_in, qb_in,
          mask_gu_in, mask_d_in, out):
    ctx = ExitStack()
    with ctx:
        def sb(name, shape, dt=F32):
            return ctx.enter_context(nc.sbuf_tensor(name, shape, dt))

        def sem(name):
            return ctx.enter_context(nc.semaphore(name))

        def dram(name, shape):
            return nc.dram_tensor(name, shape, F32, kind="Internal").ap()

        agu_g = dram("agu_gathered", [NG, 2, P, 2, 4, KT * RANK])
        bgu_g = dram("bgu_gathered", [NG, FT, 2 * RANK, NPAIR, 2 * P])
        ad_g = dram("ad_gathered", [NG, FC, P, BG, KT * RANK])
        bd_g = dram("bd_gathered", [NG, HT, 2 * RANK, NPAIR, P])
        x1_d = dram("x1_scratch", [NG, P, HT, TG])
        scale_d = dram("scale_scratch", [2, P, KT * H // P])
        weff_d = dram("weff_scratch", [P, KT, H])

        x_hi = sb("x_hi", [P, KT, TG], F32R)
        x_lo = sb("x_lo", [P, KT, TG], F32R)
        act_hi = sb("act_hi", [P, FT, TG], F32R)
        act_lo = sb("act_lo", [P, FT, TG], F32R)
        w_hi = sb("w_hi", [P, SLOTS, UNIT], F32R)
        w_lo = sb("w_lo", [P, SLOTS, UNIT], F32R)
        w_raw = sb("w_raw", [P, 2, UNIT])
        b_raw = sb("b_raw", [3 * 2 * RANK, NPAIR, 2 * P])
        b_stack = sb("b_stack", [3 * 2 * RANK, NPAIR, 2 * P], F32R)
        t_gu = sb("t_gu", [3 * 2 * RANK, 2, NPAIR, P], F32R)
        t_d = sb("t_d", [3 * 2 * RANK, NPAIR, P], F32R)
        t_masked = sb("t_masked", [P, TG])
        t_rounded = sb("t_rounded", [P, TG], F32R)
        mask_gu = sb("mask_gu", [P, TG // 2])
        mask_d = sb("mask_d", [P, TG])
        gated = sb("gated", [P, 2, TG])
        x1 = sb("x1", [P, 2, TG])
        x_raw = sb("x_raw", [P, 2, TG])
        q_w = sb("q_w", [P, QW])
        q_scale = sb("q_scale", [P, QW])
        q_recip = sb("q_recip", [P, QW])
        q_delta = sb("q_delta", [P, QW])
        q_acc = sb("q_acc", [P, QW])
        q_mask = sb("q_mask", [P, 3, QW], U8)
        q_a = sb("q_a", [LRANK, P])
        q_b = sb("q_b", [LRANK, QW])
        code = sb("code", [P, NCODE])
        small = sb("small", [P, NCODE])
        amax = sb("amax", [P, 1])
        thr = sb("thr", [P, NCODE + 1])
        idx_raw = sb("idx_raw", [1, BATCH], I32)
        idx_f = sb("idx_f", [1, 2, BATCH])
        idx = sb("idx", [1, BATCH], I32)

        def f32(ap):
            return ap.bitcast(F32)

        def bank(name):
            return ctx.enter_context(nc.psum_tensor(name, [P, TG], F32))

        gate_ps = [bank("gate_ps0"), bank("gate_ps1")]
        up_ps = [bank("up_ps0"), bank("up_ps1")]
        t_ps = bank("t_ps")
        out_ps = [bank("out_ps0"), bank("out_ps1")]
        q_ps = bank("q_ps")
        code_ps = q_ps[:, QW:QW + NCODE]

        idx_loaded, code_loaded, masks_loaded = sem("idx_loaded"), sem("code_loaded"), sem("masks_loaded")
        slog_loaded, scale_stored = sem("slog_loaded"), sem("scale_stored")
        gathered = sem("gathered")
        w_loaded = [sem("w_loaded0"), sem("w_loaded1")]
        x_loaded = [sem("x_loaded0"), sem("x_loaded1")]
        b_loaded, q_loaded = sem("b_loaded"), sem("q_loaded")
        w_rounded, w_split = sem("w_rounded"), sem("w_split")
        x_rounded, x_split = sem("x_rounded"), sem("x_split")
        b_rounded, b_split = sem("b_rounded"), sem("b_split")
        silu_done, act_rounded = sem("silu_done"), sem("act_rounded")
        prod_done, act_split, evac_done = sem("prod_done"), sem("act_split"), sem("evac_done")
        t_masked_s, t_rounded_s, t_rest_s = sem("t_masked_s"), sem("t_rounded_s"), sem("t_rest_s")
        t_hi_placed, t_lo_placed = sem("t_hi_placed"), sem("t_lo_placed")
        xsum_done = sem("xsum_done")
        x1_stored, x1_free = sem("x1_stored"), sem("x1_free")
        unit_done, x_used, delta_done = sem("unit_done"), sem("x_used"), sem("delta_done")
        q_step, weff_stored = sem("q_step"), sem("weff_stored")
        setup_step, idx_ready, code_ready, scale_ready = (sem("setup_step"), sem("idx_ready"),
                                                          sem("code_ready"), sem("scale_ready"))
        block = ctx.enter_context(nc.Block())

        N_GATHER = 4 * BG * 16

        @block.sync
        def _(sp):
            def wait(semaphore, value):
                sp.wait_ge(semaphore, value)
                sp.nop(nofuse=True)

            def load_unit(c, half, src):
                if half is not None:
                    wait(w_split, half * 2 + (c - 1))
                sp.dma_start(w_raw[:, c % 2, :], src).then_inc(w_loaded[c % 2], 16)

            def a_gu(g, s):
                return agu_g[bass.ds(g, 1), s, :, :, :, :].rearrange("a p m b n -> (a p) (m b n)")

            def a_d(g, s):
                return ad_g[bass.ds(g, 1), s, :, :, :].rearrange("a p b n -> (a p) (b n)")

            def w_eff(o):
                return weff_d[:, :, o * P:(o + 1) * P]

            def load_x(m, j, src):
                if not isinstance(m, int) or m >= 2:
                    wait(x_split, m - 1)
                sp.dma_start(x_raw[:, j % 2, :], src[:, j, :]).then_inc(x_loaded[j % 2], 16)

            def load_b(n, src, width):
                wait(b_split, n + 1)
                for c in range(3):
                    sp.dma_start(b_raw[32 * c:32 * c + 32, :, 0:width], src).then_inc(b_loaded, 16)

            def gather(g):
                with sp.Fori(0, 2) as s:
                    for b in range(4):
                        r = sp.value_load(idx[0:1, bass.ds(g * BG + s * 4 + b, 1)], min_val=0, max_val=NADAPT - 1)
                        one, pair = bass.ds(r, 1), bass.ds(s * 2 + b // 2, 1)
                        rows = slice(b % 2 * RANK, b % 2 * RANK + RANK)
                        sp.dma_start(agu_g[bass.ds(g, 1), bass.ds(s, 1), :, :, b, :].rearrange("a s p m n -> (a s p) m n"),
                                     agu_in[one, :, :, :].rearrange("a p m n -> (a p) m n")).then_inc(gathered, 16)
                        sp.dma_start(bgu_g[bass.ds(g, 1), :, rows, pair, :].rearrange("a t k c n -> (a t) (k c) n"),
                                     bgu_in[one, :, :, :].rearrange("a t k n -> (a t) k n")).then_inc(gathered, 16)
                        sp.dma_start(ad_g[bass.ds(g, 1), :, :, bass.ds(s * 4 + b, 1), :].rearrange("a t p b n -> (a t) p (b n)"),
                                     ad_in[one, :, :, :].rearrange("a t p n -> (a t) p n")).then_inc(gathered, 16)
                        sp.dma_start(bd_g[bass.ds(g, 1), :, rows, pair, :].rearrange("a t k c n -> (a t) (k c) n"),
                                     bd_in[one, :, :, :].rearrange("a t k n -> (a t) k n")).then_inc(gathered, 16)

            sp.dma_start(idx_raw[:, :], idx_in).then_inc(idx_loaded, 16)
            sp.dma_start(mask_gu[:, :], mask_gu_in).then_inc(masks_loaded, 16)
            sp.dma_start(mask_d[:, :], mask_d_in).then_inc(masks_loaded, 16)
            for j in range(2):
                load_x(j, j, x_in[0, :, :, :])
            wait(idx_ready, 1)
            gather(0)
            wait(gathered, N_GATHER)
            for s in range(2):
                load_unit(U_A + s, None, a_gu(0, s))
            for j in range(2, KT):
                load_x(j, j, x_in[0, :, :, :])
            for c in range(2):
                load_unit(U_P + c, 0, w_in[c, :, :])

            def b_source(g, n):
                if n < FT:
                    return bgu_g[bass.ds(g, 1), n, :, :, :].rearrange("a r c n -> (a r) c n")
                return bd_g[bass.ds(g, 1), n - FT, :, :, :].rearrange("a r c n -> (a r) c n")

            def ffn(g, last):
                half = g * (U_FFN // 2)
                if not last:
                    gather(g + 1)

                def before(c):
                    if 5 <= c <= 5 + 2 * NT and c % 2 == 1:
                        q = (c - 5) // 2
                        load_b(g * LN_B + q, b_source(g, q), 2 * P)
                    if 52 <= c <= 73 and (c - 52) % 3 == 0:
                        n = FT + (c - 52) // 3
                        load_b(g * LN_B + n, b_source(g, n), P)
                    if 50 <= c <= 71 and (c - 50) % 3 == 0:
                        j = (c - 50) // 3
                        if last:
                            if j == 0:
                                wait(x1_stored, 16 * HT)
                            load_x((g + 1) * KT + j, j, x1_d[0, :, :, :])
                        else:
                            load_x((g + 1) * KT + j, j, x_in[bass.ds(g + 1, 1), :, :, :].rearrange("a p k n -> (a p) k n"))

                def unit(c):
                    before(c)
                    if U_AD <= c < U_D:
                        load_unit(c, half, a_d(g, c - U_AD))
                    elif c < U_D:
                        load_unit(c, half, w_in[c - U_P, :, :])
                    elif c < U_FFN:
                        load_unit(c, half, w_in[c - U_P - FC, :, :])
                    elif last:
                        load_unit(c, half, w_eff(c - U_FFN))
                    elif c < U_FFN + U_P:
                        load_unit(c, half, a_gu(g + 1, c - U_FFN))
                    else:
                        load_unit(c, half, w_in[c - U_FFN - U_P, :, :])

                unit(4)
                unit(5)
                with sp.Fori(0, 4) as i:
                    for k in range(8):
                        if k % 2 == 1:
                            q = i * 4 + (k + 1) // 2
                            load_b(g * LN_B + q,
                                   bgu_g[bass.ds(g, 1), bass.ds(q, 1), :, :, :].rearrange("a t r c n -> (a t r) c n"), 2 * P)
                        load_unit(6 + k, half + i * 4,
                                  w_in[bass.ds(i * 8 + (6 + k - U_P), 1), :, :].rearrange("a p n -> (a p) n"))
                for c in range(38, U_FFN):
                    unit(c)
                if last:
                    wait(weff_stored, 16 * NQ)
                else:
                    wait(gathered, (g + 2) * N_GATHER)
                for c in range(U_FFN, U_FFN + SLOTS):
                    unit(c)

            def second(g, last):
                half = NG * (U_FFN // 2) + g * (HT // 2)
                m = (NG + 1) * KT + g * KT
                if not last:
                    wait(x1_stored, (g + 2) * (16 * HT))
                    src = x1_d[bass.ds(g + 1, 1), :, :, :].rearrange("a p k n -> (a p) k n")
                    load_x(m, 0, src)
                    load_x(m + 1, 1, src)
                for c in range(SLOTS, HT):
                    load_unit(c, half, w_eff(c))
                if not last:
                    for c in range(SLOTS):
                        load_unit(HT + c, half, w_eff(c))
                    for j in range(2, KT):
                        load_x(m + j, j, src)

            with sp.Fori(0, NG - 1) as g:
                ffn(g, False)
            ffn(NG - 1, True)
            with sp.Fori(0, NG - 1) as g:
                second(g, False)
            second(NG - 1, True)

        @block.gpsimd
        def _(pool):
            def wait(semaphore, value):
                pool.wait_ge(semaphore, value)
                pool.nop(nofuse=True)

            pool.sem_inc(x1_free, BUFFERS)
            pool.dma_start(code[:, :], code_in[0:1, :].to_broadcast([P, NCODE])).then_inc(code_loaded, 16)
            pool.dma_start(q_scale[:, 0:KT * H // P], slog_in).then_inc(slog_loaded, 16)
            wait(scale_ready, 1)
            pool.dma_start(scale_d[0, :, :], q_scale[:, 0:KT * H // P]).then_inc(scale_stored, 16)
            pool.dma_start(scale_d[1, :, :], q_recip[:, 0:KT * H // P]).then_inc(scale_stored, 16)
            wait(scale_stored, 32)
            scale_row = scale_d.rearrange("a p n -> a (p n)")
            weff_flat = weff_d.rearrange("p k n -> p (k n)")

            def load_piece(n, g, at, tile, width):
                pos = bass.ds(g * QCOLS + at, width)
                wait(q_step, n * QSTEPS + 1)
                pool.dma_start(q_w[:, 0:width], qw_in[:, pos]).then_inc(q_loaded, 16)
                for r, buffer in enumerate((q_scale, q_recip)):
                    pool.dma_start(buffer[:, 0:width], scale_row[r:r + 1, pos].to_broadcast([P, width])).then_inc(q_loaded, 16)
                pool.dma_start(q_a[:, :], qa_in[:, bass.ds(g * 8 + tile, 1), :].rearrange("r a n -> r (a n)")).then_inc(q_loaded, 16)
                pool.dma_start(q_b[:, 0:width], qb_in[:, bass.ds(at, width)]).then_inc(q_loaded, 16)

            def store_piece(n, g, at, width):
                wait(q_step, n * QSTEPS + (QSTEPS + 1))
                pool.dma_start(weff_flat[:, bass.ds(g * QCOLS + at, width)], q_acc[:, 0:width]).then_inc(weff_stored, 16)
                wait(weff_stored, n * 16 + 16)

            def store_x1(n, j, dst):
                wait(evac_done, n + 1 + BUFFERS)
                pool.dma_start(dst, x1[:, j % 2, :]).then_inc(x1_stored, 16)
                wait(x1_stored, n * 16 + 16)
                pool.sem_inc(x1_free, 1)

            def ffn(g):
                with pool.Fori(0, 5) as i:
                    load_piece(g * NPIECE + i, g, i * 256, i, 256)
                    store_piece(g * NPIECE + i, g, i * 256, 256)
                for it in range(2):
                    at, width = PIECES[5 + it]
                    n = g * NPIECE + 5 + it
                    load_piece(n, g, at, 5 + it, width)
                    for jj in range(4):
                        if jj == 2:
                            store_piece(n, g, at, width)
                        j = 4 * it + jj
                        store_x1(g * HT + j, j, x1_d[bass.ds(g, 1), :, j, :].rearrange("a p n -> (a p) n"))

            def second(g):
                for o in range(HT):
                    store_x1(NG * HT + g * HT + o, o, out[bass.ds(g, 1), o, :, :].rearrange("a p n -> (a p) n"))

            with pool.Fori(0, NG) as g:
                ffn(g)
            with pool.Fori(0, NG) as g:
                second(g)
            wait(x1_stored, 16 * 2 * NG * HT)

        @block.scalar
        def _(act):
            def copy(dst, src):
                return nc.scalar.activation(dst, src, ACT.Copy)

            def round_unit(c, half):
                act.wait_ge(w_loaded[c % 2], 16 * (half + (c // 2 + 1)))
                copy(w_hi[:, c % SLOTS, :], w_raw[:, c % 2, :]).then_inc(w_rounded, 1)

            def round_x(m, j, half, evac):
                act.wait_ge(x_loaded[j % 2], 16 * (half + (j // 2 + 1)))
                if evac:
                    act.wait_ge(evac_done, m - KT + 1 + BUFFERS)
                return copy(x_hi[:, j:j + 1, :] if isinstance(j, int) else x_hi[:, j, :], x_raw[:, j % 2:j % 2 + 1, :])

            def round_b(n, width):
                act.wait_ge(b_loaded, n * 48 + 48)
                copy(b_stack[:, :, 0:width], b_raw[:, :, 0:width]).then_inc(b_rounded, 1)

            def place_t(n, half_rows, dst):
                act.wait_ge(t_masked_s, n + 1)
                copy(t_rounded[:, :], t_masked[:, :]).then_inc(t_rounded_s, 1)
                act.wait_ge(t_rounded_s, n + 1)
                parts = [(c, m, p) for c in range(2) for m in range(2) for p in range(2)]
                for c, m, p in parts:
                    rows = slice(32 * (2 * m + p), 32 * (2 * m + p) + 32)
                    last = copy(dst(slice(32 * c, 32 * c + 32), m, p), f32(t_source(rows, half_rows, m, p)))
                last.then_inc(t_hi_placed, 1)

            def t_source(rows, both_sets, m, p):
                if both_sets:
                    return t_rounded[rows, :].rearrange("r (s p n) -> r s p n", s=2, p=2)[:, :, p, :]
                return t_rounded[rows, (2 * m + p) * P:(2 * m + p + 1) * P]

            def gu_dst(rows, m, p):
                return t_gu[rows, m, :, :].rearrange("r (s p) n -> r s p n", s=2)[:, :, p, :]

            def d_dst(rows, m, p):
                return t_d[rows, 2 * m + p, :]

            def silu_pair(q, k):
                act.wait_ge(act_split, q + 1)
                nc.scalar.activation(gated[:, k % 2, :], gate_ps[k % 2][:, :], ACT.Silu).then_inc(silu_done, 1)

            def round_act(q, k, dst):
                act.wait_ge(prod_done, q + 1 + BUFFERS)
                copy(dst, gated[:, k % 2:k % 2 + 1, :]).then_inc(act_rounded, 1)

            for c in range(2):
                round_x(c, c, 0, False).then_inc(x_rounded, 1)
            for c in range(2):
                round_unit(c, 0)
            for j in range(2, KT):
                round_x(j, j, 0, False).then_inc(x_rounded, 1)
            for c in range(2, SLOTS):
                round_unit(c, 0)

            def ffn(g):
                base, half = g * U_FFN, g * (U_FFN // 2)

                def done(v):
                    act.wait_ge(unit_done, base + (v + 1))

                done(0)
                round_unit(4, half)
                done(1)
                round_b(g * LN_B, 2 * P)
                place_t(2 * g, True, gu_dst)
                round_unit(5, half)
                with act.Fori(0, 5) as i:
                    for k in range(8):
                        act.wait_ge(unit_done, base + i * 8 + (3 + k))
                        if k % 2 == 1:
                            q = i * 4 + k // 2
                            silu_pair(g * FT + q, k // 2)
                            round_b(g * LN_B + q + 1, 2 * P)
                            round_act(g * FT + q, k // 2, act_hi[:, bass.ds(q, 1), :])
                        round_unit(6 + k, half + i * 4)
                done(42)
                round_unit(46, half)
                done(43)
                silu_pair(g * FT + 20, 0)
                round_b(g * LN_B + 21, 2 * P)
                round_act(g * FT + 20, 0, act_hi[:, 20:21, :])
                round_unit(47, half)
                done(44)
                act.wait_ge(act_split, g * FT + NT + 1)
                nc.scalar.activation(gated[FREST:P, 1, :], gate_ps[1][0:FREST, :], ACT.Silu).then_inc(silu_done, 1)
                act.wait_ge(prod_done, g * FT + FT + BUFFERS)
                copy(act_hi[0:FREST, NT, :], gated[0:FREST, 1, :]).then_inc(act_rounded, 1)
                round_unit(48, half)
                for v in (45, 46):
                    done(v)
                    round_unit(v + 4, half)
                done(47)
                place_t(2 * g + 1, False, d_dst)
                round_unit(51, half)
                with act.Fori(0, 2) as it:
                    for k in range(12):
                        act.wait_ge(unit_done, base + it * 12 + (U_D + 1 + k))
                        if k % 3 == 0:
                            round_b(g * LN_B + it * 4 + (FT + k // 3), P)
                        if k % 3 == 2:
                            j = it * 4 + k // 3
                            act.wait_ge(x_loaded[(k // 3) % 2], 16 * ((g + 1) * 4 + it * 2 + (k // 3 // 2 + 1)))
                            act.wait_ge(evac_done, g * HT + j + (1 + BUFFERS))
                            copy(x_hi[:, bass.ds(j, 1), :], x_raw[:, (k // 3) % 2:(k // 3) % 2 + 1, :]).then_inc(x_rounded, 1)
                        round_unit(52 + k, half + it * 6)

            def second(g, last):
                base, half = NG * U_FFN + g * HT, NG * (U_FFN // 2) + g * (HT // 2)
                m = (NG + 1) * KT + g * KT
                for v in range(HT):
                    if v == HT - 1 and not last:
                        for k in range(KT - 1):
                            act.wait_ge(x_used, g * (KT - 1) + (k + 1))
                            round_x(m + k, k, (NG + 1) * 4 + g * 4, True).then_inc(x_rounded, 1)
                    act.wait_ge(unit_done, base + (v + 1))
                    if v == HT - 1 and not last:
                        round_x(m + v, v, (NG + 1) * 4 + g * 4, True).then_inc(x_rounded, 1)
                    if v < HT - SLOTS or not last:
                        round_unit(SLOTS + v, half)

            with act.Fori(0, NG) as g:
                ffn(g)
            with act.Fori(0, NG - 1) as g:
                second(g, False)
            second(NG - 1, True)

        @block.vector
        def _(dve):
            def step(n, ins):
                ins.then_inc(setup_step, 1)
                dve.wait_ge(setup_step, n)

            for credited in (prod_done, act_split, evac_done):
                dve.sem_inc(credited, BUFFERS)
            dve.sem_inc(b_split, 1)
            dve.sem_inc(q_step, 1)

            dve.wait_ge(idx_loaded, 16)
            n = 0
            chain = []
            fa, fb = idx_f[:, 0, :], idx_f[:, 1, :]
            chain.append(lambda: nc.vector.tensor_copy(fa, idx_raw[:, :]))
            chain.append(lambda: nc.vector.tensor_scalar(fb, fa, 0.0, float(NADAPT), ALU.is_lt, ALU.mult))
            chain.append(lambda: nc.vector.tensor_tensor(fa, fa, fb, ALU.add))
            chain.append(lambda: nc.vector.tensor_scalar(fb, fa, 0.0, float(NADAPT - 1), ALU.max, ALU.min))
            for n, make in enumerate(chain):
                step(n + 1, make())
            nc.vector.tensor_copy(idx[:, :], fb).then_inc(idx_ready, 1)

            def split_unit(c, u):
                dve.wait_ge(w_rounded, u + 1)
                nc.vector.tensor_tensor(w_lo[:, c % SLOTS, :], w_raw[:, c % 2, :], f32(w_hi[:, c % SLOTS, :]),
                                        ALU.subtract).then_inc(w_split, 1)

            def split_x(m, j, at):
                dve.wait_ge(x_rounded, m + 1)
                nc.vector.tensor_tensor(x_lo[:, at, :], x_raw[:, j % 2:j % 2 + 1, :], f32(x_hi[:, at, :]),
                                        ALU.subtract).then_inc(x_split, 1)

            def split_b(n, width):
                rows = slice(2 * RANK, 4 * RANK)
                dve.wait_ge(b_rounded, n + 1)
                nc.vector.tensor_tensor(b_stack[rows, :, 0:width], b_raw[rows, :, 0:width],
                                        f32(b_stack[rows, :, 0:width]), ALU.subtract).then_inc(b_split, 1)

            for j in range(2):
                split_x(j, j, slice(j, j + 1))
            for c in range(2):
                split_unit(c, c)
            for j in range(2, KT):
                split_x(j, j, slice(j, j + 1))
            for c in range(2, SLOTS):
                split_unit(c, c)

            n = len(chain)
            dve.wait_ge(code_loaded, 16)
            chain = [
                lambda: nc.vector.tensor_scalar(small[:, :], code[:, :], -1.0, None, ALU.mult),
                lambda: nc.vector.tensor_tensor(small[:, :], small[:, :], code[:, :], ALU.max),
                lambda: nc.vector.reduce_max(amax[:, :], small[:, :], AX.X),
                lambda: nc.vector.tensor_scalar(amax[:, :], amax[:, :], 1e-8, None, ALU.max),
                lambda: nc.vector.reciprocal(amax[:, :], amax[:, :]),
                lambda: nc.vector.tensor_scalar(code[:, :], code[:, :], amax[:, 0:1], None, ALU.mult),
                lambda: nc.vector.tensor_tensor(small[:, 0:NCODE - 1], code[:, 0:NCODE - 1], code[:, 1:NCODE], ALU.add),
                lambda: nc.vector.memset(thr[:, 0:1], -3.4028235e38),
                lambda: nc.vector.memset(thr[:, NCODE:NCODE + 1], 3.4028235e38),
                lambda: nc.vector.tensor_scalar(thr[:, 1:NCODE], small[:, 0:NCODE - 1], 0.5, None, ALU.mult),
            ]
            s = NCODE // 2
            while s:
                mine, below, above = (thr[:, s:NCODE:2 * s], thr[:, 0:NCODE - s:2 * s], thr[:, 2 * s:NCODE + 1:2 * s])
                chain.append(lambda a=mine, b=below: nc.vector.tensor_tensor(a, a, b, ALU.max))
                chain.append(lambda a=mine, b=above: nc.vector.tensor_tensor(a, a, b, ALU.min))
                s //= 2
            for make in chain:
                n += 1
                step(n, make())
            nc.vector.tensor_copy(code_ps, code[:, :]).then_inc(code_ready, 1)

            dve.wait_ge(slog_loaded, 16)
            w = KT * H // P
            sx, sn, sr, sp_ = q_scale[:, 0:w], q_scale[:, w:2 * w], q_scale[:, 2 * w:3 * w], q_scale[:, 3 * w:4 * w]
            s1, s2 = q_w[:, 0:w], q_w[:, w:2 * w]
            STT = nc.vector.scalar_tensor_tensor
            chain = [
                lambda: nc.vector.tensor_scalar(sx, sx, -110.0, 92.0, ALU.max, ALU.min),
                lambda: nc.vector.tensor_scalar(sn, sx, LOG2E, None, ALU.mult),
                lambda: nc.vector.tensor_scalar(sn, sn, ROUND, ROUND, ALU.add, ALU.subtract),
                lambda: STT(sr, sn, -LN2_HI, sx, ALU.mult, ALU.add),
                lambda: STT(sr, sn, -LN2_LO, sr, ALU.mult, ALU.add),
                lambda: nc.vector.tensor_scalar(sp_, sr, EXP_POLY[0], EXP_POLY[1], ALU.mult, ALU.add),
            ]
            for coef in EXP_POLY[2:]:
                chain.append(lambda: nc.vector.tensor_tensor(sp_, sp_, sr, ALU.mult))
                chain.append(lambda c=coef: nc.vector.tensor_scalar(sp_, sp_, c, None, ALU.add))
            chain += [
                lambda: nc.vector.tensor_tensor(sp_, sp_, sr, ALU.mult),
                lambda: nc.vector.tensor_tensor(sp_, sp_, sr, ALU.mult),
                lambda: nc.vector.tensor_tensor(sp_, sp_, sr, ALU.add),
                lambda: nc.vector.tensor_scalar(sp_, sp_, 1.0, None, ALU.add),
                lambda: nc.vector.tensor_scalar(s1, sn, 0.5, None, ALU.mult),
                lambda: nc.vector.tensor_scalar(s1, s1, ROUND, ROUND, ALU.add, ALU.subtract),
                lambda: nc.vector.tensor_tensor(s2, sn, s1, ALU.subtract),
                lambda: nc.vector.tensor_scalar(s1.bitcast(I32), s1, 127.0, 8388608.0, ALU.add, ALU.mult),
                lambda: nc.vector.tensor_scalar(s2.bitcast(I32), s2, 127.0, 8388608.0, ALU.add, ALU.mult),
                lambda: nc.vector.tensor_tensor(sp_, sp_, s1, ALU.mult),
            ]
            for make in chain:
                n += 1
                step(n, make())
            step(n + 1, nc.vector.tensor_tensor(sx, sp_, s2, ALU.mult))
            nc.vector.reciprocal(q_recip[:, 0:w], sx).then_inc(scale_ready, 1)

            def piece_steps(n, width):
                delta, w, acc = q_delta[:, 0:width], q_w[:, 0:width], q_acc[:, 0:width]
                steps = []

                def add(make, after=None, before=None):
                    at = len(steps)
                    need = at if after is None else after

                    def run():
                        if before:
                            before()
                        if need > 0:
                            dve.wait_ge(q_step, n * QSTEPS + (need + 1))
                        make().then_inc(q_step, 1)
                    steps.append(run)

                def inputs():
                    dve.wait_ge(q_loaded, n * 80 + 80)
                    dve.wait_ge(delta_done, n + 1)

                add(lambda: nc.vector.tensor_scalar(delta, q_ps[:, 0:width], HALF, None, ALU.mult), before=inputs)
                add(lambda: nc.vector.tensor_tensor(w, w, delta, ALU.add))
                add(lambda: nc.vector.tensor_tensor(w, w, q_recip[:, 0:width], ALU.mult))
                add(lambda: nc.vector.tensor_copy(acc, code[:, 0:1].to_broadcast([P, width])), after=0)

                def above(i):
                    add(lambda: nc.vector.tensor_scalar(q_mask[:, i % 3, 0:width], w, thr[:, i + 1:i + 2], None,
                                                        ALU.is_gt))

                def last_mask(at):
                    dve.wait_ge(q_step, n * QSTEPS + (at + 1))
                    dve.nop(nofuse=True)

                def take(i):
                    at = len(steps)
                    add(lambda: nc.vector.copy_predicated(acc, q_mask[:, i % 3, 0:width],
                                                          code_ps[:, i + 1:i + 2].to_broadcast([P, width])),
                        after=0, before=(lambda: last_mask(at)) if i == NCODE - 2 else None)

                above(0)
                for i in range(NCODE - 1):
                    if i + 1 < NCODE - 1:
                        above(i + 1)
                    take(i)
                add(lambda: nc.vector.tensor_tensor(acc, acc, w, ALU.subtract))
                add(lambda: nc.vector.tensor_tensor(acc, acc, w, ALU.add))
                add(lambda: nc.vector.tensor_tensor(acc, acc, q_scale[:, 0:width], ALU.mult))
                add(lambda: nc.vector.tensor_tensor(acc, acc, delta, ALU.add))
                assert len(steps) == QSTEPS
                return steps

            def share(steps, k, of):
                for run in steps[QSTEPS * k // of:QSTEPS * (k + 1) // of]:
                    run()

            def place_t(n, mask, src, dst, pairs):
                nc.vector.tensor_tensor(t_masked[:, :].rearrange("p (a n) -> p a n", a=pairs),
                                        t_ps[:, :].rearrange("p (a n) -> p a n", a=pairs), mask,
                                        ALU.mult).then_inc(t_masked_s, 1)
                dve.wait_ge(t_rounded_s, n + 1)
                nc.vector.tensor_tensor(t_masked[:, :], t_masked[:, :], f32(t_rounded[:, :]),
                                        ALU.subtract).then_inc(t_rest_s, 1)
                dve.wait_ge(t_rest_s, n + 1)
                for m in range(2):
                    for p in range(2):
                        rows = slice(32 * (2 * m + p), 32 * (2 * m + p) + 32)
                        last = nc.vector.tensor_copy(dst(m, p), src(rows, m, p))
                last.then_inc(t_lo_placed, 1)

            LO = slice(4 * RANK, 6 * RANK)

            def place_gu(g):
                place_t(2 * g, mask_gu[:, :].rearrange("p (a n) -> p a n", a=1).to_broadcast([P, 2, TG // 2]),
                        lambda rows, m, p: t_masked[rows, :].rearrange("r (s p n) -> r s p n", s=2, p=2)[:, :, p, :],
                        lambda m, p: t_gu[LO, m, :, :].rearrange("r (s p) n -> r s p n", s=2)[:, :, p, :], 2)

            def place_d(g):
                place_t(2 * g + 1, mask_d[:, :].rearrange("p (a n) -> p a n", a=1),
                        lambda rows, m, p: t_masked[rows, (2 * m + p) * P:(2 * m + p + 1) * P],
                        lambda m, p: t_d[LO, 2 * m + p, :], 1)

            def product(q, k):
                dve.wait_ge(silu_done, q + 1)
                nc.vector.tensor_tensor(gated[:, k % 2, :], gated[:, k % 2, :], up_ps[k % 2][:, :],
                                        ALU.mult).then_inc(prod_done, 1)

            def split_act(q, k, at):
                dve.wait_ge(act_rounded, q + 1)
                nc.vector.tensor_tensor(act_lo[:, at, :], gated[:, k % 2:k % 2 + 1, :], f32(act_hi[:, at, :]),
                                        ALU.subtract).then_inc(act_split, 1)

            def residual(n, j, at):
                dve.wait_ge(x1_free, n + 1)
                nc.vector.tensor_tensor(x1[:, j % 2:j % 2 + 1, :], f32(x_hi[:, at, :]), f32(x_lo[:, at, :]),
                                        ALU.add).then_inc(xsum_done, 1)

            def evacuate(n, j):
                dve.wait_ge(xsum_done, n + 1)
                nc.vector.tensor_tensor(x1[:, j % 2, :], x1[:, j % 2, :], out_ps[j % 2][:, :],
                                        ALU.add).then_inc(evac_done, 1)

            dve.wait_ge(masks_loaded, 32)

            def ffn(g):
                base = g * U_FFN

                def done(v):
                    dve.wait_ge(unit_done, base + (v + 1))

                done(0)
                split_unit(4, base + 4)
                done(1)
                split_b(g * LN_B, 2 * P)
                place_gu(g)
                split_unit(5, base + 5)
                with dve.Fori(0, 5) as i:
                    steps = piece_steps(g * NPIECE + i, 256)
                    for k in range(8):
                        dve.wait_ge(unit_done, base + i * 8 + (3 + k))
                        if k % 2 == 1:
                            q = i * 4 + k // 2
                            product(g * FT + q, k // 2)
                            split_b(g * LN_B + q + 1, 2 * P)
                            split_act(g * FT + q, k // 2, bass.ds(q, 1))
                        split_unit(6 + k, base + i * 8 + (6 + k))
                        if k >= 2:
                            share(steps, k - 2, 6)
                done(42)
                split_unit(46, base + 46)
                done(43)
                product(g * FT + 20, 0)
                split_b(g * LN_B + 21, 2 * P)
                split_act(g * FT + 20, 0, slice(20, 21))
                split_unit(47, base + 47)
                done(44)
                dve.wait_ge(silu_done, g * FT + 22)
                nc.vector.tensor_tensor(gated[0:FREST, 1, :], gated[FREST:P, 1, :], gate_ps[1][FREST:P, :],
                                        ALU.mult).then_inc(prod_done, 1)
                dve.wait_ge(act_rounded, g * FT + 22)
                nc.vector.tensor_tensor(act_lo[0:FREST, NT, :], gated[0:FREST, 1, :],
                                        f32(act_hi[0:FREST, NT, :]), ALU.subtract).then_inc(act_split, 1)
                split_unit(48, base + 48)
                for v in (45, 46):
                    done(v)
                    split_unit(v + 4, base + v + 4)
                done(47)
                place_d(g)
                split_unit(51, base + 51)
                with dve.Fori(0, 2) as it:
                    steps = piece_steps(g * NPIECE + it + 5, PIECES[5][1])
                    for k in range(12):
                        j = it * 4 + k // 3
                        if k % 3 == 2:
                            residual(g * HT + j, k // 3, bass.ds(j, 1))
                        dve.wait_ge(unit_done, base + it * 12 + (U_D + 1 + k))
                        if k % 3 == 0:
                            split_b(g * LN_B + FT + j, P)
                        if k % 3 == 2:
                            evacuate(g * HT + j, k // 3)
                            split_x((g + 1) * KT + j, k // 3, bass.ds(j, 1))
                        split_unit(52 + k, base + it * 12 + (52 + k))
                        if 2 <= k < 8:
                            share(steps, k - 2, 6)

            def second(g, last):
                base = NG * U_FFN + g * HT
                m = (NG + 1) * KT + g * KT
                for v in range(HT):
                    n = NG * HT + g * HT + v
                    if v == HT - 1 and not last:
                        for k in range(KT - 1):
                            split_x(m + k, k, slice(k, k + 1))
                    residual(n, v, slice(v, v + 1))
                    dve.wait_ge(unit_done, base + (v + 1))
                    evacuate(n, v)
                    if v == HT - 1 and not last:
                        split_x(m + v, v, slice(v, v + 1))
                    if v < HT - SLOTS or not last:
                        split_unit(SLOTS + v, base + SLOTS + v)

            with dve.Fori(0, NG) as g:
                ffn(g)
            with dve.Fori(0, NG - 1) as g:
                second(g, False)
            second(NG - 1, True)

        @block.tensor
        def _(pe):
            mm = nc.tensor.matmul

            def three(out_ap, w_hi_ap, w_lo_ap, m_hi, m_lo, start, stop=False):
                mm(out_ap, w_hi_ap, m_hi, start=start, stop=False)
                mm(out_ap, w_hi_ap, m_lo, start=False, stop=False)
                return mm(out_ap, w_lo_ap, m_hi, start=False, stop=stop)

            def unit(slot, out_ap, moving, start=True, stop=False, tiles=KT, wait=None, mark=None):
                for k in range(tiles):
                    if wait:
                        wait(k)
                    m_hi, m_lo = moving(k)
                    n = m_hi.shape[0]
                    cols = slice(k * P, (k + 1) * P)
                    last = three(out_ap, w_hi[0:n, slot, cols], w_lo[0:n, slot, cols], m_hi, m_lo,
                                 start and k == 0, stop and k == tiles - 1)
                    if mark:
                        mark(k, last)
                return last

            def x_moving(k):
                return x_hi[:, k, :], x_lo[:, k, :]

            def lora(out_tile, b_ap, t_ap, stop=True):
                for pair in range(NPAIR):
                    last = mm(out_tile[:, pair * P:(pair + 1) * P], b_ap[:, pair, :], t_ap[:, pair, :],
                              start=False, stop=stop and pair == NPAIR - 1)
                return last

            def delta(n, width):
                pe.wait_ge(q_loaded, n * 80 + 80)
                mm(q_ps[:, 0:width], q_a[:, :], q_b[:, 0:width], start=True, stop=True).then_inc(delta_done, 1)

            def pair(base, c, q, k, n_b):
                pe.wait_ge(w_split, base + c + 1)
                pe.wait_ge(prod_done, q + 1)
                unit(c % SLOTS, gate_ps[k % 2][:, :], x_moving)
                pe.wait_ge(b_split, n_b + 2)
                lora(gate_ps[k % 2], b_stack[:, :, 0:P], t_gu[:, 0, :, :]).then_inc(unit_done, 1)

            def pair_up(base, c, k):
                pe.wait_ge(w_split, base + c + 1)
                unit(c % SLOTS, up_ps[k % 2][:, :], x_moving)
                lora(up_ps[k % 2], b_stack[:, :, P:2 * P], t_gu[:, 1, :, :]).then_inc(unit_done, 1)

            def ffn(g):
                base = g * U_FFN
                for s in range(2):
                    pe.wait_ge(w_split, base + s + 1)
                    cols = slice(s * TG // 2, (s + 1) * TG // 2)
                    for k in range(KT):
                        if s == 0:
                            pe.wait_ge(x_split, g * KT + (k + 1))
                        last = three(t_ps[:, cols], w_hi[:, s, k::KT], w_lo[:, s, k::KT], x_hi[:, k, cols],
                                     x_lo[:, k, cols], k == 0, k == KT - 1)
                    last.then_inc(unit_done, 1)
                with pe.Fori(0, 5) as i:
                    for k in range(8):
                        if k == 2:
                            delta(g * NPIECE + i, 256)
                        if k == 0:
                            pe.wait_ge(t_hi_placed, 2 * g + 1)
                            pe.wait_ge(t_lo_placed, 2 * g + 1)
                        if k % 2 == 0:
                            pair(base + i * 8, 2 + k, g * FT + i * 4 + k // 2, k // 2, g * LN_B + i * 4 + k // 2)
                        else:
                            pair_up(base + i * 8, 2 + k, k // 2)
                pair(base, 42, g * FT + 20, 0, g * LN_B + 20)
                pair_up(base, 43, 0)
                pe.wait_ge(w_split, base + U_M + 1)
                pe.wait_ge(prod_done, g * FT + NT + 1)
                unit(U_M % SLOTS, gate_ps[1][:, :], x_moving)
                pe.wait_ge(b_split, g * LN_B + FT + 1)
                lora(gate_ps[1], b_stack[:, :, 0:P], t_gu[:, 0, :, :], stop=False)
                lora(gate_ps[1], b_stack[:, :, P:2 * P], t_gu[:, 1, :, :]).then_inc(unit_done, 1)

                def act_moving(t):
                    rows = FREST if t == NT else P
                    return act_hi[0:rows, t, :], act_lo[0:rows, t, :]

                for s in range(FC):
                    c = U_AD + s
                    pe.wait_ge(w_split, base + c + 1)
                    for k in range(min(KT, FT - s * KT)):
                        t = s * KT + k
                        m_hi, m_lo = act_moving(t)
                        n = m_hi.shape[0]
                        pe.wait_ge(act_split, g * FT + (t + 1 + BUFFERS))
                        last = three(t_ps[:, :], w_hi[0:n, c % SLOTS, k::KT], w_lo[0:n, c % SLOTS, k::KT], m_hi, m_lo,
                                     t == 0, t == FT - 1)
                    last.then_inc(unit_done, 1)
                with pe.Fori(0, 2) as it:
                    for k in range(12):
                        c = U_D + k
                        jj = k // 3
                        s = k % 3
                        n = g * HT + it * 4 + jj
                        pe.wait_ge(w_split, base + it * 12 + (c + 1))
                        if s == 0:
                            pe.wait_ge(evac_done, n + 1)
                        last = unit(c % SLOTS, out_ps[jj % 2][:, :], lambda k: act_moving(s * KT + k), start=s == 0,
                                    tiles=min(KT, FT - s * KT))
                        if s == 2:
                            if k == 2:
                                pe.wait_ge(t_hi_placed, 2 * g + 2)
                                pe.wait_ge(t_lo_placed, 2 * g + 2)
                            pe.wait_ge(b_split, g * LN_B + it * 4 + (FT + jj + 2))
                            last = lora(out_ps[jj % 2], b_stack[:, :, 0:P], t_d[:, :, :])
                        last.then_inc(unit_done, 1)
                        if k == 1:
                            delta(g * NPIECE + it + 5, PIECES[5][1])

            def second(g):
                base = NG * U_FFN + g * HT
                for o in range(HT):
                    pe.wait_ge(w_split, base + o + 1)
                    pe.wait_ge(evac_done, g * HT + (NG * HT + o + 1))

                    def wait(k):
                        pe.wait_ge(x_split, NG * KT + g * KT + (k + 1))

                    def mark(k, last):
                        if k < KT - 1:
                            last.then_inc(x_used, 1)

                    unit(o % SLOTS, out_ps[o % 2][:, :], x_moving, stop=True, wait=wait if o == 0 else None,
                         mark=mark if o == HT - 1 else None).then_inc(unit_done, 1)

            with pe.Fori(0, NG) as g:
                ffn(g)
            with pe.Fori(0, NG) as g:
                second(g)


def kernel(**inputs):
    import numpy as np
    import concourse.bacc as bacc
    from concourse.bass_utils import run_bass_kernel_spmd

    def tiles(w, n_k, n_m):
        return w.reshape(n_m, -1, n_k, P).transpose(0, 3, 2, 1)

    def padded(a, axis, size):
        shape = list(a.shape)
        shape[axis] = size - shape[axis]
        return np.concatenate([a, np.zeros(shape, a.dtype)], axis)

    x = np.asarray(inputs["x"])
    w_gate, w_up, w_down = (np.asarray(inputs[f"L0_cond_W_{n}"]) for n in ("gate", "up", "down"))
    a_gate, a_up, a_down = (np.asarray(inputs[f"L0_cond_A_{n}"])[0] for n in ("gate", "up", "down"))
    b_gate, b_up, b_down = (np.asarray(inputs[f"L0_cond_B_{n}"])[0] for n in ("gate", "up", "down"))
    whole = NT * P
    FP = FC * KT * P

    gate, up = tiles(w_gate[:whole], KT, NT), tiles(w_up[:whole], KT, NT)
    rest = tiles(np.concatenate([w_gate[whole:], w_up[whole:]]), KT, 1)
    down = padded(w_down, 1, FP).reshape(HT, P, FC, KT, P).transpose(0, 2, 4, 3, 1)
    units = np.concatenate([np.stack([gate, up], 1).reshape(2 * NT, P, UNIT), rest.reshape(1, P, UNIT),
                            down.reshape(HT * FC, P, UNIT)])
    agu = np.stack([a_gate, a_up], 1).reshape(NADAPT, 2, RANK, KT, P).transpose(0, 4, 1, 2, 3)
    bt_gate, bt_up = b_gate.transpose(0, 2, 1), b_up.transpose(0, 2, 1)
    zero = np.zeros((NADAPT, RANK, FREST), b_gate.dtype)
    side = [np.concatenate([bt_gate[:, :, :whole], bt_gate[:, :, whole:], zero], 2),
            np.concatenate([bt_up[:, :, :whole], zero, bt_up[:, :, whole:]], 2)]
    bgu = np.stack(side, 2).reshape(NADAPT, RANK, 2, FT, P).transpose(0, 3, 1, 2, 4)
    ad = padded(a_down, 2, FP).reshape(NADAPT, RANK, FC, KT, P).transpose(0, 2, 4, 1, 3)
    bd = b_down.transpose(0, 2, 1).reshape(NADAPT, RANK, HT, P).transpose(0, 2, 1, 3)
    lora_a, lora_b = np.asarray(inputs["L1_cond_lora_A"]), np.asarray(inputs["L1_cond_lora_B"])
    qa = np.repeat(lora_a.reshape(LRANK, KT, 1, P), 4, 2)
    qb = np.concatenate([lora_b.T, lora_b.T], 1)

    rows, cols = np.arange(P)[:, None], np.arange(TG)[None, :]
    arrays = {
        "x_in": x.reshape(NG, TG, KT, P).transpose(0, 3, 2, 1),
        "idx_in": np.asarray(inputs["itok_B_2_6"]).reshape(1, BATCH),
        "code_in": np.asarray(inputs["condB_codebook"]).reshape(1, NCODE),
        "w_in": units,
        "agu_in": agu.reshape(NADAPT, P, 2, RANK * KT),
        "bgu_in": bgu.reshape(NADAPT, FT, RANK, 2 * P),
        "ad_in": ad.reshape(NADAPT, FC, P, RANK * KT),
        "bd_in": bd,
        "qw_in": np.asarray(inputs["L1_cond_weight"]).reshape(H, KT, P).transpose(2, 1, 0).reshape(P, KT * H),
        "slog_in": np.asarray(inputs["L1_cond_scale_log"]).reshape(H, KT).T.reshape(P, KT * H // P),
        "qa_in": qa.reshape(LRANK, 4 * KT, P),
        "qb_in": qb,
        "mask_gu_in": np.where(rows % 64 // RANK == cols[:, :TG // 2] // SEQ, 0.5, 0.0).astype(np.float32),
        "mask_d_in": np.where(rows // RANK == cols // SEQ, 0.5, 0.0).astype(np.float32),
    }
    nc = bacc.Bacc("TRN2", target_bir_lowering=False, num_devices=1)
    arrays = {n: np.ascontiguousarray(a) for n, a in arrays.items()}
    aps = {n: nc.dram_tensor(n, a.shape, mybir.dt.from_np(a.dtype), kind="ExternalInput").ap()
           for n, a in arrays.items()}
    out = nc.dram_tensor("out", [NG, HT, P, TG], F32, kind="ExternalOutput").ap()
    build(nc, **aps, out=out)
    got = run_bass_kernel_spmd(nc, [arrays], core_ids=[0]).results[0]["out"]
    return np.ascontiguousarray(np.asarray(got).transpose(0, 3, 1, 2)).reshape(BATCH, SEQ, H)
```

```python
import concourse.bass as bass
from concourse import mybir
from contextlib import ExitStack

F32 = mybir.dt.float32
F32R = mybir.dt.float32r
I32 = mybir.dt.int32
U8 = mybir.dt.uint8
ALU = mybir.AluOpType
ACT = mybir.ActivationFunctionType
AX = mybir.AxisListType

P = 128
BATCH, SEQ, H = 32, 64, 1024
F = 2752
RANK, NADAPT = 16, 16
LRANK = 64
NCODE = 32
TG = 512
NG = BATCH * SEQ // TG
BG = TG // SEQ
NPAIR = BG // 2
KT = H // P
NT = F // P
FREST = F - NT * P
FT = NT + 1
FC = 3
HT = H // P
UNIT = KT * P

U_A, U_P = 0, 2
U_M = U_P + 2 * NT
U_AD = U_M + 1
U_D = U_AD + FC
U_FFN = U_D + FC * HT
SLOTS = 4
LN_B = FT + HT

PIECES = [(256 * i, 256) for i in range(5)] + [(1280, 384), (1664, 384)]
QCOLS = sum(w for _, w in PIECES)
QW = max(w for _, w in PIECES)
NQ = len(PIECES) * NG
assert QCOLS * NG == KT * H and U_FFN % SLOTS == 0
NPIECE = len(PIECES)
BUFFERS = 2
MID = NCODE // 2
QSTEPS = 5 + 2 * (NCODE - 1) + 4

HALF = float(0.5)
LOG2E = 1.4426950408889634
LN2_HI, LN2_LO = 0.693359375, -2.12194440e-4
EXP_POLY = [1.9875691500e-4, 1.3981999507e-3, 8.3334519073e-3, 4.1665795894e-2, 1.6666665459e-1,
            5.0000001201e-1]
ROUND = 12582912.0


def build(nc, x_in, idx_in, code_in, w_in, agu_in, bgu_in, ad_in, bd_in, qw_in, slog_in, qa_in, qb_in,
          mask_gu_in, mask_d_in, out):
    ctx = ExitStack()
    with ctx:
        def sb(name, shape, dt=F32):
            return ctx.enter_context(nc.sbuf_tensor(name, shape, dt))

        def sem(name):
            return ctx.enter_context(nc.semaphore(name))

        def dram(name, shape):
            return nc.dram_tensor(name, shape, F32, kind="Internal").ap()

        agu_g = dram("agu_gathered", [NG, 2, P, 2, 4, KT * RANK])
        bgu_g = dram("bgu_gathered", [NG, FT, 2 * RANK, NPAIR, 2 * P])
        ad_g = dram("ad_gathered", [NG, FC, P, BG, KT * RANK])
        bd_g = dram("bd_gathered", [NG, HT, 2 * RANK, NPAIR, P])
        x1_d = dram("x1_scratch", [NG, P, HT, TG])
        scale_d = dram("scale_scratch", [2, P, KT * H // P])
        weff_d = dram("weff_scratch", [P, KT, H])

        x_hi = sb("x_hi", [P, KT, TG], F32R)
        x_lo = sb("x_lo", [P, KT, TG], F32R)
        act_hi = sb("act_hi", [P, FT, TG], F32R)
        act_lo = sb("act_lo", [P, FT, TG], F32R)
        w_hi = sb("w_hi", [P, SLOTS, UNIT], F32R)
        w_lo = sb("w_lo", [P, SLOTS, UNIT], F32R)
        w_raw = sb("w_raw", [P, 2, UNIT])
        b_raw = sb("b_raw", [3 * 2 * RANK, NPAIR, 2 * P])
        b_stack = sb("b_stack", [3 * 2 * RANK, NPAIR, 2 * P], F32R)
        t_gu = sb("t_gu", [3 * 2 * RANK, 2, NPAIR, P], F32R)
        t_d = sb("t_d", [3 * 2 * RANK, NPAIR, P], F32R)
        t_masked = sb("t_masked", [P, TG])
        t_rounded = sb("t_rounded", [P, TG], F32R)
        mask_gu = sb("mask_gu", [P, BG // 2])
        mask_d = sb("mask_d", [P, BG])
        gated = sb("gated", [P, 2, TG])
        x1 = sb("x1", [P, 2, TG])
        x_raw = sb("x_raw", [P, 2, TG])
        q_w = sb("q_w", [P, QW])
        q_scale = sb("q_scale", [P, QW])
        q_recip = sb("q_recip", [P, QW])
        q_value = sb("q_value", [P, QW])
        q_out = sb("q_out", [P, QW])
        q_delta = sb("q_delta", [P, QW])
        q_acc = sb("q_acc", [P, QW])
        q_acc2 = sb("q_acc2", [P, QW])
        q_mask = sb("q_mask", [P, 6, QW], U8)
        q_a = sb("q_a", [LRANK, P])
        q_b = sb("q_b", [LRANK, QW])
        code = sb("code", [P, NCODE])
        small = sb("small", [P, NCODE])
        amax = sb("amax", [P, 1])
        thr = sb("thr", [P, NCODE + 1])
        idx_raw = sb("idx_raw", [1, BATCH], I32)
        idx_f = sb("idx_f", [1, 2, BATCH])
        idx = sb("idx", [1, BATCH], I32)

        def f32(ap):
            return ap.bitcast(F32)

        def bank(name):
            return ctx.enter_context(nc.psum_tensor(name, [P, TG], F32))

        gate_ps = [bank("gate_ps0"), bank("gate_ps1")]
        up_ps = [bank("up_ps0"), bank("up_ps1")]
        t_ps = bank("t_ps")
        out_ps = [bank("out_ps0"), bank("out_ps1")]
        code_ps = bank("code_ps")[:, 0:NCODE]

        idx_loaded, code_loaded, masks_loaded = sem("idx_loaded"), sem("code_loaded"), sem("masks_loaded")
        slog_loaded, scale_stored = sem("slog_loaded"), sem("scale_stored")
        a_gathered, b_gathered, d_gathered = sem("a_gathered"), sem("b_gathered"), sem("d_gathered")
        w_loaded = [sem("w_loaded0"), sem("w_loaded1")]
        x_loaded = [sem("x_loaded0"), sem("x_loaded1")]
        b_loaded, q_loaded, q_ab_loaded = sem("b_loaded"), sem("q_loaded"), sem("q_ab_loaded")
        q_scale_loaded = sem("q_scale_loaded")
        w_rounded, w_split = sem("w_rounded"), sem("w_split")
        x_rounded, x_split = sem("x_rounded"), sem("x_split")
        b_rounded, b_split = sem("b_rounded"), sem("b_split")
        silu_done, act_rounded = sem("silu_done"), sem("act_rounded")
        prod_done, act_split, evac_done = sem("prod_done"), sem("act_split"), sem("evac_done")
        t_masked_s, t_rounded_s, t_rest_s = sem("t_masked_s"), sem("t_rounded_s"), sem("t_rest_s")
        t_hi_placed, t_lo_placed = sem("t_hi_placed"), sem("t_lo_placed")
        xsum_done = sem("xsum_done")
        x1_stored, x1_free = sem("x1_stored"), sem("x1_free")
        unit_done, x_used, delta_done = sem("unit_done"), sem("x_used"), sem("delta_done")
        q_step, weff_stored, piece_stored = sem("q_step"), sem("weff_stored"), sem("piece_stored")
        setup_step, idx_ready, code_ready, scale_ready = (sem("setup_step"), sem("idx_ready"),
                                                          sem("code_ready"), sem("scale_ready"))

        def loop(engine, end):
            return nc.Fori(0, end, engines=[engine.engine], hint_back_edge=True)

        block = ctx.enter_context(nc.Block())

        @block.sync
        def _(sp):
            def wait(semaphore, value):
                sp.wait_ge(semaphore, value)
                sp.nop(nofuse=True)

            def load_unit(c, half, src):
                if half is not None:
                    wait(w_split, half * 2 + (c - 1))
                sp.dma_start(w_raw[:, c % 2, :], src).then_inc(w_loaded[c % 2], 16)

            def a_gu(g, s):
                return agu_g[bass.ds(g, 1), s, :, :, :, :].rearrange("a p m b n -> (a p) (m b n)")

            def a_d(g, s):
                return ad_g[bass.ds(g, 1), s, :, :, :].rearrange("a p b n -> (a p) (b n)")

            def w_eff(o):
                return weff_d[:, :, o * P:(o + 1) * P]

            def load_x(m, j, src):
                if not isinstance(m, int) or m >= 2:
                    wait(x_split, m - 1)
                sp.dma_start(x_raw[:, j % 2, :], src[:, j, :]).then_inc(x_loaded[j % 2], 16)

            def load_b(n, src, width):
                wait(b_split, n + 1)
                for c in range(3):
                    sp.dma_start(b_raw[32 * c:32 * c + 32, :, 0:width], src).then_inc(b_loaded, 16)

            def adapter(g, b):
                return bass.ds(sp.value_load(idx[0:1, bass.ds(g * BG + b, 1)], min_val=0, max_val=NADAPT - 1), 1)

            def gather_a(g, s, b, one):
                sp.dma_start(agu_g[bass.ds(g, 1), bass.ds(s, 1), :, :, b, :].rearrange("a s p m n -> (a s p) m n"),
                             agu_in[one, :, :, :].rearrange("a p m n -> (a p) m n")).then_inc(a_gathered, 16)

            def gather_b(g, s, b, one):
                rows, pair = slice(b % 2 * RANK, b % 2 * RANK + RANK), bass.ds(s * 2 + b // 2, 1)
                sp.dma_start(bgu_g[bass.ds(g, 1), :, rows, pair, :].rearrange("a t k c n -> (a t) (k c) n"),
                             bgu_in[one, :, :, :].rearrange("a t k n -> (a t) k n")).then_inc(b_gathered, 16)

            def gather_d(g, s, b, one):
                rows, pair = slice(b % 2 * RANK, b % 2 * RANK + RANK), bass.ds(s * 2 + b // 2, 1)
                sp.dma_start(ad_g[bass.ds(g, 1), :, :, bass.ds(s * 4 + b, 1), :].rearrange("a t p b n -> (a t) p (b n)"),
                             ad_in[one, :, :, :].rearrange("a t p n -> (a t) p n")).then_inc(d_gathered, 16)
                sp.dma_start(bd_g[bass.ds(g, 1), :, rows, pair, :].rearrange("a t k c n -> (a t) (k c) n"),
                             bd_in[one, :, :, :].rearrange("a t k n -> (a t) k n")).then_inc(d_gathered, 16)

            sp.dma_start(idx_raw[:, :], idx_in).then_inc(idx_loaded, 16)
            for j in range(2):
                load_x(j, j, x_in[0, :, :, :])
            wait(idx_ready, 1)
            for b in range(BG):
                gather_a(0, b // 4, b % 4, adapter(0, b))
            for b in range(BG):
                gather_b(0, b // 4, b % 4, adapter(0, b))
            wait(a_gathered, 16 * BG)
            for s in range(2):
                load_unit(U_A + s, None, a_gu(0, s))
            for j in range(2, KT):
                load_x(j, j, x_in[0, :, :, :])
            for c in range(2):
                load_unit(U_P + c, 0, w_in[c, :, :])
            for b in range(BG):
                gather_d(0, b // 4, b % 4, adapter(0, b))

            def b_source(g, n):
                if n < FT:
                    return bgu_g[bass.ds(g, 1), n, :, :, :].rearrange("a r c n -> (a r) c n")
                return bd_g[bass.ds(g, 1), n - FT, :, :, :].rearrange("a r c n -> (a r) c n")

            def ffn(g, last):
                half = g * (U_FFN // 2)

                def before(c):
                    if 5 <= c <= 5 + 2 * NT and c % 2 == 1:
                        q = (c - 5) // 2
                        load_b(g * LN_B + q, b_source(g, q), 2 * P)
                    if 52 <= c <= 73 and (c - 52) % 3 == 0:
                        n = FT + (c - 52) // 3
                        load_b(g * LN_B + n, b_source(g, n), P)
                    if 50 <= c <= 71 and (c - 50) % 3 == 0:
                        j = (c - 50) // 3
                        if last:
                            if j == 0:
                                wait(x1_stored, 16 * HT)
                            load_x((g + 1) * KT + j, j, x1_d[0, :, :, :])
                        else:
                            load_x((g + 1) * KT + j, j, x_in[bass.ds(g + 1, 1), :, :, :].rearrange("a p k n -> (a p) k n"))

                def unit(c):
                    before(c)
                    if U_AD <= c < U_D:
                        load_unit(c, half, a_d(g, c - U_AD))
                    elif c < U_D:
                        load_unit(c, half, w_in[c - U_P, :, :])
                    elif c < U_FFN:
                        load_unit(c, half, w_in[c - U_P - FC, :, :])
                    elif last:
                        load_unit(c, half, w_eff(c - U_FFN))
                    elif c < U_FFN + U_P:
                        load_unit(c, half, a_gu(g + 1, c - U_FFN))
                    else:
                        load_unit(c, half, w_in[c - U_FFN - U_P, :, :])

                unit(4)
                wait(b_gathered, (g + 1) * (16 * BG))
                unit(5)
                wait(d_gathered, (g + 1) * (2 * 16 * BG))
                with loop(sp, 2) as i:
                    for k in range(16):
                        if k % 4 == 2 and not last:
                            one = adapter(g + 1, i * 4 + k // 4)
                            gather_a(g + 1, i, k // 4, one)
                            gather_b(g + 1, i, k // 4, one)
                            gather_d(g + 1, i, k // 4, one)
                        if k % 2 == 1:
                            q = i * 8 + (k + 1) // 2
                            load_b(g * LN_B + q,
                                   bgu_g[bass.ds(g, 1), bass.ds(q, 1), :, :, :].rearrange("a t r c n -> (a t r) c n"), 2 * P)
                        load_unit(6 + k, half + i * 8,
                                  w_in[bass.ds(i * 16 + (6 + k - U_P), 1), :, :].rearrange("a p n -> (a p) n"))
                for c in range(38, U_FFN):
                    unit(c)
                if not last:
                    wait(a_gathered, (g + 2) * (16 * BG))
                for c in range(U_FFN, U_FFN + SLOTS):
                    if last:
                        wait_w_eff(c - U_FFN)
                    unit(c)

            def wait_w_eff(o):
                after = sum(at % H >= (o + 1) * P for at, _ in PIECES[-2:])
                wait(weff_stored, 16 * (NQ - after))

            def second(g, last):
                half = NG * (U_FFN // 2) + g * (HT // 2)
                m = (NG + 1) * KT + g * KT
                if not last:
                    wait(x1_stored, (g + 2) * (16 * HT))
                    src = x1_d[bass.ds(g + 1, 1), :, :, :].rearrange("a p k n -> (a p) k n")
                    load_x(m, 0, src)
                    load_x(m + 1, 1, src)
                for c in range(SLOTS, HT):
                    wait_w_eff(c)
                    load_unit(c, half, w_eff(c))
                if not last:
                    for c in range(SLOTS):
                        load_unit(HT + c, half, w_eff(c))
                    for j in range(2, KT):
                        load_x(m + j, j, src)

            with loop(sp, NG - 1) as g:
                ffn(g, False)
            ffn(NG - 1, True)
            with loop(sp, NG - 1) as g:
                second(g, False)
            second(NG - 1, True)

        @block.gpsimd
        def _(pool):
            def wait(semaphore, value):
                pool.wait_ge(semaphore, value)
                pool.nop(nofuse=True)

            def load_adapter(g, i):
                at, width = PIECES[i]
                pool.dma_start(q_a[:, :], qa_in[:, bass.ds(g * 8 + at // 256, 1), :].rearrange("r a n -> r (a n)")).then_inc(q_ab_loaded, 16)
                pool.dma_start(q_b[:, 0:width], qb_in[:, at:at + width]).then_inc(q_ab_loaded, 16)

            pool.sem_inc(x1_free, BUFFERS)
            pool.sem_inc(piece_stored, 1)
            load_adapter(0, 0)
            pool.dma_start(code[:, :], code_in[0:1, :].to_broadcast([P, NCODE])).then_inc(code_loaded, 16)
            pool.dma_start(q_scale[:, 0:KT * H // P], slog_in).then_inc(slog_loaded, 16)
            pool.dma_start(mask_gu[:, :], mask_gu_in).then_inc(masks_loaded, 16)
            pool.dma_start(mask_d[:, :], mask_d_in).then_inc(masks_loaded, 16)
            wait(scale_ready, 1)
            pool.dma_start(scale_d[0, :, :], q_scale[:, 0:KT * H // P]).then_inc(scale_stored, 16)
            pool.dma_start(scale_d[1, :, :], q_recip[:, 0:KT * H // P]).then_inc(scale_stored, 16)
            wait(scale_stored, 32)
            scale_row = scale_d.rearrange("a p n -> a (p n)")
            weff_flat = weff_d.rearrange("p k n -> p (k n)")

            def row(g, i, r):
                at, width = PIECES[i]
                return scale_row[r:r + 1, bass.ds(g * QCOLS + at, width)].to_broadcast([P, width])

            def load_piece(g, i):
                at, width = PIECES[i]
                pool.dma_start(q_w[:, 0:width], qw_in[:, bass.ds(g * QCOLS + at, width)]).then_inc(q_loaded, 16)
                pool.dma_start(q_recip[:, 0:width], row(g, i, 1)).then_inc(q_loaded, 16)

            def load_scale(g, i):
                pool.dma_start(q_scale[:, 0:PIECES[i][1]], row(g, i, 0)).then_inc(q_scale_loaded, 16)

            def store_x1(n, j, dst):
                wait(evac_done, n + 1 + BUFFERS)
                pool.dma_start(dst, x1[:, j % 2, :]).then_inc(x1_stored, 16)
                wait(x1_stored, n * 16 + 16)
                pool.sem_inc(x1_free, 1)

            def piece(g, last, i):
                n, (at, width) = g * NPIECE + i, PIECES[i]
                more, after = i + 1 < NPIECE or not last, (g, i + 1) if i + 1 < NPIECE else (g + 1, 0)
                if more:
                    wait(delta_done, n + 1)
                    load_adapter(*after)
                    wait(q_step, n * QSTEPS + (3 + QSTEPS))
                    load_piece(*after)
                wait(q_step, n * QSTEPS + 2 * QSTEPS)
                if more:
                    load_scale(*after)
                pool.dma_start(weff_flat[:, bass.ds(g * QCOLS + at, width)], q_out[:, 0:width]).then_inc(weff_stored, 16)
                wait(weff_stored, n * 16 + 16)
                pool.sem_inc(piece_stored, 1)

            def ffn(g, last):
                for i in range(5):
                    piece(g, last, i)
                for j in range(HT):
                    store_x1(g * HT + j, j, x1_d[bass.ds(g, 1), :, j, :].rearrange("a p n -> (a p) n"))
                    if j % 4 == 3:
                        piece(g, last, 5 + j // 4)

            def second(g):
                for o in range(HT):
                    store_x1(NG * HT + g * HT + o, o, out[bass.ds(g, 1), o, :, :].rearrange("a p n -> (a p) n"))

            load_piece(0, 0)
            load_scale(0, 0)
            with loop(pool, NG - 1) as g:
                ffn(g, False)
            ffn(NG - 1, True)
            with loop(pool, NG) as g:
                second(g)
            wait(x1_stored, 16 * 2 * NG * HT)

        @block.scalar
        def _(act):
            def copy(dst, src):
                return nc.scalar.activation(dst, src, ACT.Copy)

            def round_unit(c, half):
                act.wait_ge(w_loaded[c % 2], 16 * (half + (c // 2 + 1)))
                copy(w_hi[:, c % SLOTS, :], w_raw[:, c % 2, :]).then_inc(w_rounded, 1)

            def round_x(m, j, half, evac):
                act.wait_ge(x_loaded[j % 2], 16 * (half + (j // 2 + 1)))
                if evac:
                    act.wait_ge(evac_done, m - KT + 1 + BUFFERS)
                return copy(x_hi[:, j:j + 1, :] if isinstance(j, int) else x_hi[:, j, :], x_raw[:, j % 2:j % 2 + 1, :])

            def round_b(n, width):
                act.wait_ge(b_loaded, n * 48 + 48)
                copy(b_stack[:, :, 0:width], b_raw[:, :, 0:width]).then_inc(b_rounded, 1)

            def place_t(n, half_rows, dst):
                act.wait_ge(t_masked_s, n + 1)
                copy(t_rounded[:, :], t_masked[:, :]).then_inc(t_rounded_s, 1)
                act.wait_ge(t_rounded_s, n + 1)
                parts = [(c, m, p) for c in range(2) for m in range(2) for p in range(2)]
                for c, m, p in parts:
                    rows = slice(32 * (2 * m + p), 32 * (2 * m + p) + 32)
                    last = copy(dst(slice(32 * c, 32 * c + 32), m, p), f32(t_source(rows, half_rows, m, p)))
                last.then_inc(t_hi_placed, 1)

            def t_source(rows, both_sets, m, p):
                if both_sets:
                    return t_rounded[rows, :].rearrange("r (s p n) -> r s p n", s=2, p=2)[:, :, p, :]
                return t_rounded[rows, (2 * m + p) * P:(2 * m + p + 1) * P]

            def gu_dst(rows, m, p):
                return t_gu[rows, m, :, :].rearrange("r (s p) n -> r s p n", s=2)[:, :, p, :]

            def d_dst(rows, m, p):
                return t_d[rows, 2 * m + p, :]

            def silu_pair(q, k):
                act.wait_ge(act_split, q + 1)
                nc.scalar.activation(gated[:, k % 2, :], gate_ps[k % 2][:, :], ACT.Silu).then_inc(silu_done, 1)

            def round_act(q, k, dst):
                act.wait_ge(prod_done, q + 1 + BUFFERS)
                copy(dst, gated[:, k % 2:k % 2 + 1, :]).then_inc(act_rounded, 1)

            for c in range(2):
                round_x(c, c, 0, False).then_inc(x_rounded, 1)
            for c in range(2):
                round_unit(c, 0)
            for j in range(2, KT):
                round_x(j, j, 0, False).then_inc(x_rounded, 1)
            for c in range(2, SLOTS):
                round_unit(c, 0)

            def ffn(g):
                base, half = g * U_FFN, g * (U_FFN // 2)

                def done(v):
                    act.wait_ge(unit_done, base + (v + 1))

                done(0)
                round_unit(4, half)
                done(1)
                round_b(g * LN_B, 2 * P)
                place_t(2 * g, True, gu_dst)
                round_unit(5, half)
                with loop(act, 5) as i:
                    for k in range(8):
                        act.wait_ge(unit_done, base + i * 8 + (3 + k))
                        if k % 2 == 1:
                            q = i * 4 + k // 2
                            silu_pair(g * FT + q, k // 2)
                            round_b(g * LN_B + q + 1, 2 * P)
                            round_act(g * FT + q, k // 2, act_hi[:, bass.ds(q, 1), :])
                        round_unit(6 + k, half + i * 4)
                done(42)
                round_unit(46, half)
                done(43)
                silu_pair(g * FT + 20, 0)
                round_b(g * LN_B + 21, 2 * P)
                round_act(g * FT + 20, 0, act_hi[:, 20:21, :])
                round_unit(47, half)
                done(44)
                act.wait_ge(act_split, g * FT + NT + 1)
                nc.scalar.activation(gated[FREST:P, 1, :], gate_ps[1][0:FREST, :], ACT.Silu).then_inc(silu_done, 1)
                act.wait_ge(prod_done, g * FT + FT + BUFFERS)
                copy(act_hi[0:FREST, NT, :], gated[0:FREST, 1, :]).then_inc(act_rounded, 1)
                round_unit(48, half)
                for v in (45, 46):
                    done(v)
                    round_unit(v + 4, half)
                done(47)
                place_t(2 * g + 1, False, d_dst)
                round_unit(51, half)
                with loop(act, 2) as it:
                    for k in range(12):
                        act.wait_ge(unit_done, base + it * 12 + (U_D + 1 + k))
                        if k % 3 == 0:
                            round_b(g * LN_B + it * 4 + (FT + k // 3), P)
                        if k % 3 == 2:
                            j = it * 4 + k // 3
                            act.wait_ge(x_loaded[(k // 3) % 2], 16 * ((g + 1) * 4 + it * 2 + (k // 3 // 2 + 1)))
                            act.wait_ge(evac_done, g * HT + j + (1 + BUFFERS))
                            copy(x_hi[:, bass.ds(j, 1), :], x_raw[:, (k // 3) % 2:(k // 3) % 2 + 1, :]).then_inc(x_rounded, 1)
                        round_unit(52 + k, half + it * 6)

            def second(g, last):
                base, half = NG * U_FFN + g * HT, NG * (U_FFN // 2) + g * (HT // 2)
                m = (NG + 1) * KT + g * KT
                for v in range(HT):
                    if v == HT - 1 and not last:
                        for k in range(KT - 1):
                            act.wait_ge(x_used, g * (KT - 1) + (k + 1))
                            round_x(m + k, k, (NG + 1) * 4 + g * 4, True).then_inc(x_rounded, 1)
                    act.wait_ge(unit_done, base + (v + 1))
                    if v == HT - 1 and not last:
                        round_x(m + v, v, (NG + 1) * 4 + g * 4, True).then_inc(x_rounded, 1)
                    if v < HT - SLOTS or not last:
                        round_unit(SLOTS + v, half)

            with loop(act, NG) as g:
                ffn(g)
            with loop(act, NG - 1) as g:
                second(g, False)
            second(NG - 1, True)

        @block.vector
        def _(dve):
            def step(n, ins):
                ins.then_inc(setup_step, 1)
                dve.wait_ge(setup_step, n)

            for credited in (prod_done, act_split, evac_done):
                dve.sem_inc(credited, BUFFERS)
            dve.sem_inc(b_split, 1)
            dve.sem_inc(q_step, QSTEPS)

            dve.wait_ge(idx_loaded, 16)
            n = 0
            chain = []
            fa, fb = idx_f[:, 0, :], idx_f[:, 1, :]
            chain.append(lambda: nc.vector.tensor_copy(fa, idx_raw[:, :]))
            chain.append(lambda: nc.vector.tensor_scalar(fb, fa, 0.0, float(NADAPT), ALU.is_lt, ALU.mult))
            chain.append(lambda: nc.vector.tensor_tensor(fa, fa, fb, ALU.add))
            chain.append(lambda: nc.vector.tensor_scalar(fb, fa, 0.0, float(NADAPT - 1), ALU.max, ALU.min))
            for n, make in enumerate(chain):
                step(n + 1, make())
            nc.vector.tensor_copy(idx[:, :], fb).then_inc(idx_ready, 1)

            def split_unit(c, u):
                dve.wait_ge(w_rounded, u + 1)
                nc.vector.tensor_tensor(w_lo[:, c % SLOTS, :], w_raw[:, c % 2, :], f32(w_hi[:, c % SLOTS, :]),
                                        ALU.subtract).then_inc(w_split, 1)

            def split_x(m, j, at):
                dve.wait_ge(x_rounded, m + 1)
                nc.vector.tensor_tensor(x_lo[:, at, :], x_raw[:, j % 2:j % 2 + 1, :], f32(x_hi[:, at, :]),
                                        ALU.subtract).then_inc(x_split, 1)

            def split_b(n, width):
                rows = slice(2 * RANK, 4 * RANK)
                dve.wait_ge(b_rounded, n + 1)
                nc.vector.tensor_tensor(b_stack[rows, :, 0:width], b_raw[rows, :, 0:width],
                                        f32(b_stack[rows, :, 0:width]), ALU.subtract).then_inc(b_split, 1)

            for j in range(2):
                split_x(j, j, slice(j, j + 1))
            for c in range(2):
                split_unit(c, c)
            for j in range(2, KT):
                split_x(j, j, slice(j, j + 1))
            for c in range(2, SLOTS):
                split_unit(c, c)

            n = len(chain)
            dve.wait_ge(code_loaded, 16)
            chain = [
                lambda: nc.vector.tensor_scalar(small[:, :], code[:, :], -1.0, None, ALU.mult),
                lambda: nc.vector.tensor_tensor(small[:, :], small[:, :], code[:, :], ALU.max),
                lambda: nc.vector.reduce_max(amax[:, :], small[:, :], AX.X),
                lambda: nc.vector.tensor_scalar(amax[:, :], amax[:, :], 1e-8, None, ALU.max),
                lambda: nc.vector.reciprocal(amax[:, :], amax[:, :]),
                lambda: nc.vector.tensor_scalar(code[:, :], code[:, :], amax[:, 0:1], None, ALU.mult),
                lambda: nc.vector.tensor_tensor(small[:, 0:NCODE - 1], code[:, 0:NCODE - 1], code[:, 1:NCODE], ALU.add),
                lambda: nc.vector.memset(thr[:, 0:1], -3.4028235e38),
                lambda: nc.vector.memset(thr[:, NCODE:NCODE + 1], 3.4028235e38),
                lambda: nc.vector.tensor_scalar(thr[:, 1:NCODE], small[:, 0:NCODE - 1], 0.5, None, ALU.mult),
            ]
            s = NCODE // 2
            while s:
                mine, below, above = (thr[:, s:NCODE:2 * s], thr[:, 0:NCODE - s:2 * s], thr[:, 2 * s:NCODE + 1:2 * s])
                chain.append(lambda a=mine, b=below: nc.vector.tensor_tensor(a, a, b, ALU.max))
                chain.append(lambda a=mine, b=above: nc.vector.tensor_tensor(a, a, b, ALU.min))
                s //= 2
            for make in chain:
                n += 1
                step(n, make())
            nc.vector.tensor_copy(code_ps, code[:, :]).then_inc(code_ready, 1)

            dve.wait_ge(slog_loaded, 16)
            w = KT * H // P
            sx, sn, sr, sp_ = q_scale[:, 0:w], q_scale[:, w:2 * w], q_scale[:, 2 * w:3 * w], q_scale[:, 3 * w:4 * w]
            s1, s2 = q_w[:, 0:w], q_w[:, w:2 * w]
            STT = nc.vector.scalar_tensor_tensor
            chain = [
                lambda: nc.vector.tensor_scalar(sx, sx, -110.0, 92.0, ALU.max, ALU.min),
                lambda: nc.vector.tensor_scalar(sn, sx, LOG2E, None, ALU.mult),
                lambda: nc.vector.tensor_scalar(sn, sn, ROUND, ROUND, ALU.add, ALU.subtract),
                lambda: STT(sr, sn, -LN2_HI, sx, ALU.mult, ALU.add),
                lambda: STT(sr, sn, -LN2_LO, sr, ALU.mult, ALU.add),
                lambda: nc.vector.tensor_scalar(sp_, sr, EXP_POLY[0], EXP_POLY[1], ALU.mult, ALU.add),
            ]
            for coef in EXP_POLY[2:]:
                chain.append(lambda: nc.vector.tensor_tensor(sp_, sp_, sr, ALU.mult))
                chain.append(lambda c=coef: nc.vector.tensor_scalar(sp_, sp_, c, None, ALU.add))
            chain += [
                lambda: nc.vector.tensor_tensor(sp_, sp_, sr, ALU.mult),
                lambda: nc.vector.tensor_tensor(sp_, sp_, sr, ALU.mult),
                lambda: nc.vector.tensor_tensor(sp_, sp_, sr, ALU.add),
                lambda: nc.vector.tensor_scalar(sp_, sp_, 1.0, None, ALU.add),
                lambda: nc.vector.tensor_scalar(s1, sn, 0.5, None, ALU.mult),
                lambda: nc.vector.tensor_scalar(s1, s1, ROUND, ROUND, ALU.add, ALU.subtract),
                lambda: nc.vector.tensor_tensor(s2, sn, s1, ALU.subtract),
                lambda: nc.vector.tensor_scalar(s1.bitcast(I32), s1, 127.0, 8388608.0, ALU.add, ALU.mult),
                lambda: nc.vector.tensor_scalar(s2.bitcast(I32), s2, 127.0, 8388608.0, ALU.add, ALU.mult),
                lambda: nc.vector.tensor_tensor(sp_, sp_, s1, ALU.mult),
            ]
            for make in chain:
                n += 1
                step(n, make())
            step(n + 1, nc.vector.tensor_tensor(sx, sp_, s2, ALU.mult))
            nc.vector.reciprocal(q_recip[:, 0:w], sx).then_inc(scale_ready, 1)

            def piece_steps(n, width):
                delta, w, acc = q_delta[:, 0:width], q_value[:, 0:width], q_acc[:, 0:width]
                steps = []

                def add(make, after=None, before=None):
                    at = len(steps)
                    need = at if after is None else after

                    def run():
                        if before:
                            before()
                        if need > 0 or at == 0:
                            dve.wait_ge(q_step, n * QSTEPS + (need + QSTEPS))
                        make().then_inc(q_step, 1)
                    steps.append(run)

                def inputs():
                    dve.wait_ge(q_loaded, n * 32 + 32)
                    dve.wait_ge(delta_done, n + 1)

                add(lambda: nc.vector.tensor_scalar(delta, t_ps[:, 0:width], HALF, None, ALU.mult), before=inputs)
                add(lambda: nc.vector.tensor_tensor(w, q_w[:, 0:width], delta, ALU.add))
                add(lambda: nc.vector.tensor_tensor(w, w, q_recip[:, 0:width], ALU.mult))
                add(lambda: nc.vector.tensor_copy(q_acc2[:, 0:width], code[:, MID:MID + 1].to_broadcast([P, width])),
                    after=0)
                add(lambda: nc.vector.tensor_copy(acc, code[:, 0:1].to_broadcast([P, width])), after=0)

                chains = ((acc, 0), (q_acc2[:, 0:width], MID))

                def above(chain, i, after):
                    first = chains[chain][1]
                    add(lambda: nc.vector.tensor_scalar(q_mask[:, 2 * (i % 3) + chain, 0:width], w,
                                                        thr[:, first + i + 1:first + i + 2], None, ALU.is_gt), after=after)

                def take(chain, i, before=None):
                    target, first = chains[chain]
                    code_of = code_ps[:, first + i + 1:first + i + 2]
                    add(lambda: nc.vector.copy_predicated(target, q_mask[:, 2 * (i % 3) + chain, 0:width],
                                                          code_of.to_broadcast([P, width])), after=0, before=before)

                def settle():
                    at = len(steps)

                    def run():
                        dve.wait_ge(q_step, n * QSTEPS + (at + QSTEPS))
                        dve.nop(nofuse=True)
                    return run

                above(0, 0, len(steps))
                above(1, 0, 0)
                for i in range(MID - 1):
                    if i + 1 < MID - 1:
                        above(0, i + 1, 0)
                        above(1, i + 1, len(steps) - 1)
                        take(0, i)
                    else:
                        take(0, i, settle())
                    take(1, i)
                add(lambda: nc.vector.tensor_scalar(q_mask[:, 2 * ((MID - 1) % 3), 0:width], w,
                                                    thr[:, MID:MID + 1], None, ALU.is_gt))
                add(lambda: nc.vector.copy_predicated(acc, q_mask[:, 2 * ((MID - 1) % 3), 0:width],
                                                      q_acc2[:, 0:width]), after=0, before=settle())
                add(lambda: nc.vector.tensor_tensor(acc, acc, w, ALU.subtract))
                add(lambda: nc.vector.tensor_tensor(acc, acc, w, ALU.add))
                add(lambda: nc.vector.tensor_tensor(acc, acc, q_scale[:, 0:width], ALU.mult),
                    before=lambda: dve.wait_ge(q_scale_loaded, n * 16 + 16))
                add(lambda: nc.vector.tensor_tensor(q_out[:, 0:width], acc, delta, ALU.add),
                    before=lambda: dve.wait_ge(piece_stored, n + 1))
                assert len(steps) == QSTEPS
                return steps

            def share(steps, k, of):
                for run in steps[QSTEPS * k // of:QSTEPS * (k + 1) // of]:
                    run()

            def place_t(n, mask, src, dst, sets):
                shape = dict(a=sets, n=SEQ)
                nc.vector.tensor_tensor(t_masked[:, :].rearrange("p (a m n) -> p a m n", **shape),
                                        t_ps[:, :].rearrange("p (a m n) -> p a m n", **shape),
                                        mask.to_broadcast([P, sets, BG // sets, SEQ]),
                                        ALU.mult).then_inc(t_masked_s, 1)
                dve.wait_ge(t_rounded_s, n + 1)
                nc.vector.tensor_tensor(t_masked[:, :], t_masked[:, :], f32(t_rounded[:, :]),
                                        ALU.subtract).then_inc(t_rest_s, 1)
                dve.wait_ge(t_rest_s, n + 1)
                for m in range(2):
                    for p in range(2):
                        rows = slice(32 * (2 * m + p), 32 * (2 * m + p) + 32)
                        last = nc.vector.tensor_copy(dst(m, p), src(rows, m, p))
                last.then_inc(t_lo_placed, 1)

            LO = slice(4 * RANK, 6 * RANK)

            def place_gu(g):
                place_t(2 * g, mask_gu[:, :].rearrange("p (a m n) -> p a m n", a=1, n=1),
                        lambda rows, m, p: t_masked[rows, :].rearrange("r (s p n) -> r s p n", s=2, p=2)[:, :, p, :],
                        lambda m, p: t_gu[LO, m, :, :].rearrange("r (s p) n -> r s p n", s=2)[:, :, p, :], 2)

            def place_d(g):
                place_t(2 * g + 1, mask_d[:, :].rearrange("p (a m n) -> p a m n", a=1, n=1),
                        lambda rows, m, p: t_masked[rows, (2 * m + p) * P:(2 * m + p + 1) * P],
                        lambda m, p: t_d[LO, 2 * m + p, :], 1)

            def product(q, k):
                dve.wait_ge(silu_done, q + 1)
                nc.vector.tensor_tensor(gated[:, k % 2, :], gated[:, k % 2, :], up_ps[k % 2][:, :],
                                        ALU.mult).then_inc(prod_done, 1)

            def split_act(q, k, at):
                dve.wait_ge(act_rounded, q + 1)
                nc.vector.tensor_tensor(act_lo[:, at, :], gated[:, k % 2:k % 2 + 1, :], f32(act_hi[:, at, :]),
                                        ALU.subtract).then_inc(act_split, 1)

            def residual(n, j, at):
                dve.wait_ge(x1_free, n + 1)
                nc.vector.tensor_tensor(x1[:, j % 2:j % 2 + 1, :], f32(x_hi[:, at, :]), f32(x_lo[:, at, :]),
                                        ALU.add).then_inc(xsum_done, 1)

            def evacuate(n, j):
                dve.wait_ge(xsum_done, n + 1)
                nc.vector.tensor_tensor(x1[:, j % 2, :], x1[:, j % 2, :], out_ps[j % 2][:, :],
                                        ALU.add).then_inc(evac_done, 1)

            dve.wait_ge(masks_loaded, 32)

            def ffn(g):
                base = g * U_FFN

                def done(v):
                    dve.wait_ge(unit_done, base + (v + 1))

                done(0)
                split_unit(4, base + 4)
                done(1)
                split_b(g * LN_B, 2 * P)
                place_gu(g)
                split_unit(5, base + 5)
                with loop(dve, 5) as i:
                    steps = piece_steps(g * NPIECE + i, 256)
                    for k in range(8):
                        dve.wait_ge(unit_done, base + i * 8 + (3 + k))
                        if k % 2 == 1:
                            q = i * 4 + k // 2
                            product(g * FT + q, k // 2)
                            split_b(g * LN_B + q + 1, 2 * P)
                            split_act(g * FT + q, k // 2, bass.ds(q, 1))
                        split_unit(6 + k, base + i * 8 + (6 + k))
                        share(steps, k, 8)
                done(42)
                split_unit(46, base + 46)
                done(43)
                product(g * FT + 20, 0)
                split_b(g * LN_B + 21, 2 * P)
                split_act(g * FT + 20, 0, slice(20, 21))
                split_unit(47, base + 47)
                done(44)
                dve.wait_ge(silu_done, g * FT + 22)
                nc.vector.tensor_tensor(gated[0:FREST, 1, :], gated[FREST:P, 1, :], gate_ps[1][FREST:P, :],
                                        ALU.mult).then_inc(prod_done, 1)
                dve.wait_ge(act_rounded, g * FT + 22)
                nc.vector.tensor_tensor(act_lo[0:FREST, NT, :], gated[0:FREST, 1, :],
                                        f32(act_hi[0:FREST, NT, :]), ALU.subtract).then_inc(act_split, 1)
                split_unit(48, base + 48)
                for v in (45, 46):
                    done(v)
                    split_unit(v + 4, base + v + 4)
                done(47)
                place_d(g)
                split_unit(51, base + 51)
                with loop(dve, 2) as it:
                    steps = piece_steps(g * NPIECE + it + 5, PIECES[5][1])
                    for k in range(12):
                        j = it * 4 + k // 3
                        if k % 3 == 2:
                            residual(g * HT + j, k // 3, bass.ds(j, 1))
                        dve.wait_ge(unit_done, base + it * 12 + (U_D + 1 + k))
                        if k % 3 == 0:
                            split_b(g * LN_B + FT + j, P)
                        if k % 3 == 2:
                            evacuate(g * HT + j, k // 3)
                            split_x((g + 1) * KT + j, k // 3, bass.ds(j, 1))
                        split_unit(52 + k, base + it * 12 + (52 + k))
                        share(steps, k, 12)

            def second(g, last):
                base = NG * U_FFN + g * HT
                m = (NG + 1) * KT + g * KT
                for v in range(HT):
                    n = NG * HT + g * HT + v
                    if v == HT - 1 and not last:
                        for k in range(KT - 1):
                            split_x(m + k, k, slice(k, k + 1))
                    residual(n, v, slice(v, v + 1))
                    dve.wait_ge(unit_done, base + (v + 1))
                    evacuate(n, v)
                    if v == HT - 1 and not last:
                        split_x(m + v, v, slice(v, v + 1))
                    if v < HT - SLOTS or not last:
                        split_unit(SLOTS + v, base + SLOTS + v)

            with loop(dve, NG) as g:
                ffn(g)
            with loop(dve, NG - 1) as g:
                second(g, False)
            second(NG - 1, True)

        @block.tensor
        def _(pe):
            mm = nc.tensor.matmul

            def three(out_ap, w_hi_ap, w_lo_ap, m_hi, m_lo, start, stop=False):
                mm(out_ap, w_hi_ap, m_hi, start=start, stop=False)
                mm(out_ap, w_hi_ap, m_lo, start=False, stop=False)
                return mm(out_ap, w_lo_ap, m_hi, start=False, stop=stop)

            def unit(slot, out_ap, moving, start=True, stop=False, tiles=KT, wait=None, mark=None):
                for k in range(tiles):
                    if wait:
                        wait(k)
                    m_hi, m_lo = moving(k)
                    n = m_hi.shape[0]
                    cols = slice(k * P, (k + 1) * P)
                    last = three(out_ap, w_hi[0:n, slot, cols], w_lo[0:n, slot, cols], m_hi, m_lo,
                                 start and k == 0, stop and k == tiles - 1)
                    if mark:
                        mark(k, last)
                return last

            def x_moving(k):
                return x_hi[:, k, :], x_lo[:, k, :]

            def lora(out_tile, b_ap, t_ap, stop=True):
                for pair in range(NPAIR):
                    last = mm(out_tile[:, pair * P:(pair + 1) * P], b_ap[:, pair, :], t_ap[:, pair, :],
                              start=False, stop=stop and pair == NPAIR - 1)
                return last

            def delta(n, width, read):
                pe.wait_ge(t_masked_s, read)
                pe.wait_ge(q_ab_loaded, n * 32 + 32)
                pe.wait_ge(q_step, n * QSTEPS + 1)
                mm(t_ps[:, 0:width], q_a[:, :], q_b[:, 0:width], start=True, stop=True).then_inc(delta_done, 1)

            def pair(base, c, q, k, n_b, first=None):
                pe.wait_ge(w_split, base + c + 1)
                pe.wait_ge(prod_done, q + 1)
                unit(c % SLOTS, gate_ps[k % 2][:, :], x_moving)
                pe.wait_ge(b_split, n_b + 2)
                if first is not None:
                    pe.wait_ge(t_hi_placed, 2 * first + 1)
                    pe.wait_ge(t_lo_placed, 2 * first + 1)
                lora(gate_ps[k % 2], b_stack[:, :, 0:P], t_gu[:, 0, :, :]).then_inc(unit_done, 1)

            def pair_up(base, c, k):
                pe.wait_ge(w_split, base + c + 1)
                unit(c % SLOTS, up_ps[k % 2][:, :], x_moving)
                lora(up_ps[k % 2], b_stack[:, :, P:2 * P], t_gu[:, 1, :, :]).then_inc(unit_done, 1)

            def ffn(g):
                base = g * U_FFN
                for s in range(2):
                    pe.wait_ge(w_split, base + s + 1)
                    cols = slice(s * TG // 2, (s + 1) * TG // 2)
                    for k in range(KT):
                        if s == 0:
                            pe.wait_ge(x_split, g * KT + (k + 1))
                        last = three(t_ps[:, cols], w_hi[:, s, k::KT], w_lo[:, s, k::KT], x_hi[:, k, cols],
                                     x_lo[:, k, cols], k == 0, k == KT - 1)
                    last.then_inc(unit_done, 1)
                with loop(pe, 5) as i:
                    for k in range(8):
                        if k == 1:
                            delta(g * NPIECE + i, 256, 2 * g + 1)
                        if k % 2 == 0:
                            pair(base + i * 8, 2 + k, g * FT + i * 4 + k // 2, k // 2, g * LN_B + i * 4 + k // 2,
                                 g if k == 0 else None)
                        else:
                            pair_up(base + i * 8, 2 + k, k // 2)
                pair(base, 42, g * FT + 20, 0, g * LN_B + 20)
                pair_up(base, 43, 0)
                pe.wait_ge(w_split, base + U_M + 1)
                pe.wait_ge(prod_done, g * FT + NT + 1)
                unit(U_M % SLOTS, gate_ps[1][:, :], x_moving)
                pe.wait_ge(b_split, g * LN_B + FT + 1)
                lora(gate_ps[1], b_stack[:, :, 0:P], t_gu[:, 0, :, :], stop=False)
                lora(gate_ps[1], b_stack[:, :, P:2 * P], t_gu[:, 1, :, :]).then_inc(unit_done, 1)

                def act_moving(t):
                    rows = FREST if t == NT else P
                    return act_hi[0:rows, t, :], act_lo[0:rows, t, :]

                for s in range(FC):
                    c = U_AD + s
                    pe.wait_ge(w_split, base + c + 1)
                    for k in range(min(KT, FT - s * KT)):
                        t = s * KT + k
                        m_hi, m_lo = act_moving(t)
                        n = m_hi.shape[0]
                        pe.wait_ge(act_split, g * FT + (t + 1 + BUFFERS))
                        last = three(t_ps[:, :], w_hi[0:n, c % SLOTS, k::KT], w_lo[0:n, c % SLOTS, k::KT], m_hi, m_lo,
                                     t == 0, t == FT - 1)
                    last.then_inc(unit_done, 1)
                with loop(pe, 2) as it:
                    for k in range(12):
                        c = U_D + k
                        jj = k // 3
                        s = k % 3
                        n = g * HT + it * 4 + jj
                        pe.wait_ge(w_split, base + it * 12 + (c + 1))
                        if s == 0:
                            pe.wait_ge(evac_done, n + 1)
                        last = unit(c % SLOTS, out_ps[jj % 2][:, :], lambda k: act_moving(s * KT + k), start=s == 0,
                                    tiles=min(KT, FT - s * KT))
                        if s == 2:
                            if k == 2:
                                pe.wait_ge(t_hi_placed, 2 * g + 2)
                                pe.wait_ge(t_lo_placed, 2 * g + 2)
                            pe.wait_ge(b_split, g * LN_B + it * 4 + (FT + jj + 2))
                            last = lora(out_ps[jj % 2], b_stack[:, :, 0:P], t_d[:, :, :])
                        last.then_inc(unit_done, 1)
                        if k == 1:
                            delta(g * NPIECE + it + 5, PIECES[5][1], 2 * g + 2)

            def second(g):
                base = NG * U_FFN + g * HT
                for o in range(HT):
                    pe.wait_ge(w_split, base + o + 1)
                    pe.wait_ge(evac_done, g * HT + (NG * HT + o + 1))

                    def wait(k):
                        pe.wait_ge(x_split, NG * KT + g * KT + (k + 1))

                    def mark(k, last):
                        if k < KT - 1:
                            last.then_inc(x_used, 1)

                    unit(o % SLOTS, out_ps[o % 2][:, :], x_moving, stop=True, wait=wait if o == 0 else None,
                         mark=mark if o == HT - 1 else None).then_inc(unit_done, 1)

            with loop(pe, NG) as g:
                ffn(g)
            with loop(pe, NG) as g:
                second(g)


def kernel(**inputs):
    import numpy as np
    import concourse.bacc as bacc
    from concourse.bass_utils import run_bass_kernel_spmd

    def tiles(w, n_k, n_m):
        return w.reshape(n_m, -1, n_k, P).transpose(0, 3, 2, 1)

    def padded(a, axis, size):
        shape = list(a.shape)
        shape[axis] = size - shape[axis]
        return np.concatenate([a, np.zeros(shape, a.dtype)], axis)

    x = np.asarray(inputs["x"])
    w_gate, w_up, w_down = (np.asarray(inputs[f"L0_cond_W_{n}"]) for n in ("gate", "up", "down"))
    a_gate, a_up, a_down = (np.asarray(inputs[f"L0_cond_A_{n}"])[0] for n in ("gate", "up", "down"))
    b_gate, b_up, b_down = (np.asarray(inputs[f"L0_cond_B_{n}"])[0] for n in ("gate", "up", "down"))
    whole = NT * P
    FP = FC * KT * P

    gate, up = tiles(w_gate[:whole], KT, NT), tiles(w_up[:whole], KT, NT)
    rest = tiles(np.concatenate([w_gate[whole:], w_up[whole:]]), KT, 1)
    down = padded(w_down, 1, FP).reshape(HT, P, FC, KT, P).transpose(0, 2, 4, 3, 1)
    units = np.concatenate([np.stack([gate, up], 1).reshape(2 * NT, P, UNIT), rest.reshape(1, P, UNIT),
                            down.reshape(HT * FC, P, UNIT)])
    agu = np.stack([a_gate, a_up], 1).reshape(NADAPT, 2, RANK, KT, P).transpose(0, 4, 1, 2, 3)
    bt_gate, bt_up = b_gate.transpose(0, 2, 1), b_up.transpose(0, 2, 1)
    zero = np.zeros((NADAPT, RANK, FREST), b_gate.dtype)
    side = [np.concatenate([bt_gate[:, :, :whole], bt_gate[:, :, whole:], zero], 2),
            np.concatenate([bt_up[:, :, :whole], zero, bt_up[:, :, whole:]], 2)]
    bgu = np.stack(side, 2).reshape(NADAPT, RANK, 2, FT, P).transpose(0, 3, 1, 2, 4)
    ad = padded(a_down, 2, FP).reshape(NADAPT, RANK, FC, KT, P).transpose(0, 2, 4, 1, 3)
    bd = b_down.transpose(0, 2, 1).reshape(NADAPT, RANK, HT, P).transpose(0, 2, 1, 3)
    lora_a, lora_b = np.asarray(inputs["L1_cond_lora_A"]), np.asarray(inputs["L1_cond_lora_B"])
    qa = np.repeat(lora_a.reshape(LRANK, KT, 1, P), 4, 2)
    qb = np.concatenate([lora_b.T, lora_b.T], 1)

    rows, cols = np.arange(P)[:, None], np.arange(BG)[None, :]
    arrays = {
        "x_in": x.reshape(NG, TG, KT, P).transpose(0, 3, 2, 1),
        "idx_in": np.asarray(inputs["itok_B_2_6"]).reshape(1, BATCH),
        "code_in": np.asarray(inputs["condB_codebook"]).reshape(1, NCODE),
        "w_in": units,
        "agu_in": agu.reshape(NADAPT, P, 2, RANK * KT),
        "bgu_in": bgu.reshape(NADAPT, FT, RANK, 2 * P),
        "ad_in": ad.reshape(NADAPT, FC, P, RANK * KT),
        "bd_in": bd,
        "qw_in": np.asarray(inputs["L1_cond_weight"]).reshape(H, KT, P).transpose(2, 1, 0).reshape(P, KT * H),
        "slog_in": np.asarray(inputs["L1_cond_scale_log"]).reshape(H, KT).T.reshape(P, KT * H // P),
        "qa_in": qa.reshape(LRANK, 4 * KT, P),
        "qb_in": qb,
        "mask_gu_in": np.where(rows % 64 // RANK == cols[:, :BG // 2], 0.5, 0.0).astype(np.float32),
        "mask_d_in": np.where(rows // RANK == cols, 0.5, 0.0).astype(np.float32),
    }
    nc = bacc.Bacc("TRN2", target_bir_lowering=False, num_devices=1)
    arrays = {n: np.ascontiguousarray(a) for n, a in arrays.items()}
    aps = {n: nc.dram_tensor(n, a.shape, mybir.dt.from_np(a.dtype), kind="ExternalInput").ap()
           for n, a in arrays.items()}
    out = nc.dram_tensor("out", [NG, HT, P, TG], F32, kind="ExternalOutput").ap()
    build(nc, **aps, out=out)
    got = run_bass_kernel_spmd(nc, [arrays], core_ids=[0]).results[0]["out"]
    return np.ascontiguousarray(np.asarray(got).transpose(0, 3, 1, 2)).reshape(BATCH, SEQ, H)
```

```python
import concourse.bass as bass
from concourse import mybir
from contextlib import ExitStack

F32 = mybir.dt.float32
F32R = mybir.dt.float32r
I32 = mybir.dt.int32
U8 = mybir.dt.uint8
ALU = mybir.AluOpType
ACT = mybir.ActivationFunctionType
AX = mybir.AxisListType

P = 128
BATCH, SEQ, H = 32, 64, 1024
F = 2752
RANK, NADAPT = 16, 16
LRANK = 64
NCODE = 32
TG = 512
NG = BATCH * SEQ // TG
BG = TG // SEQ
NPAIR = BG // 2
KT = H // P
NT = F // P
FREST = F - NT * P
FT = NT + 1
FC = 3
HT = H // P
UNIT = KT * P

U_G0, U_A, U_UP0, U_P = 0, 1, 3, 2
U_M = U_P + 2 * NT
MORE_LOADS = BG // 2 - 1
U_AD = U_M + 1
U_D = U_AD + FC
U_FFN = U_D + FC * HT
SLOTS = 4
LN_B = FT + HT

PIECES = [(256 * i, 256) for i in range(5)] + [(1280, 384), (1664, 384)]
QCOLS = sum(w for _, w in PIECES)
QW = max(w for _, w in PIECES)
NQ = len(PIECES) * NG
assert QCOLS * NG == KT * H and U_FFN % SLOTS == 0
NPIECE = len(PIECES)
BUFFERS = 2
MID = NCODE // 2
QSTEPS = 5 + 2 * (NCODE - 1) + 4
EXP_STEPS = 27

HALF = float(0.5)
LOG2E = 1.4426950408889634
LN2_HI, LN2_LO = 0.693359375, -2.12194440e-4
EXP_POLY = [1.9875691500e-4, 1.3981999507e-3, 8.3334519073e-3, 4.1665795894e-2, 1.6666665459e-1,
            5.0000001201e-1]
ROUND = 12582912.0


def build(nc, x_in, idx_in, code_in, w_in, agu_in, bgu_in, ad_in, bd_in, qw_in, slog_in, qa_in, qb_in,
          mask_gu_in, mask_d_in, out):
    ctx = ExitStack()
    with ctx:
        def sb(name, shape, dt=F32):
            return ctx.enter_context(nc.sbuf_tensor(name, shape, dt))

        def sem(name):
            return ctx.enter_context(nc.semaphore(name))

        def dram(name, shape):
            return nc.dram_tensor(name, shape, F32, kind="Internal").ap()

        agu_g = dram("agu_gathered", [NG, 2, P, 2, 4, KT * RANK])
        bgu_g = dram("bgu_gathered", [NG, FT, 2 * RANK, NPAIR, 2 * P])
        ad_g = dram("ad_gathered", [NG, FC, P, BG, KT * RANK])
        bd_g = dram("bd_gathered", [NG, HT, 2 * RANK, NPAIR, P])
        x1_d = dram("x1_scratch", [NG, P, HT, TG])
        scale_d = dram("scale_scratch", [2, P, KT * H // P])
        weff_d = dram("weff_scratch", [P, KT, H])

        x_hi = sb("x_hi", [P, KT, TG], F32R)
        x_lo = sb("x_lo", [P, KT, TG], F32R)
        act_hi = sb("act_hi", [P, FT, TG], F32R)
        act_lo = sb("act_lo", [P, FT, TG], F32R)
        w_hi = sb("w_hi", [P, SLOTS, UNIT], F32R)
        w_lo = sb("w_lo", [P, SLOTS, UNIT], F32R)
        w_raw = sb("w_raw", [P, 2, UNIT])
        b_raw = sb("b_raw", [3 * 2 * RANK, NPAIR, 2 * P])
        b_stack = sb("b_stack", [3 * 2 * RANK, NPAIR, 2 * P], F32R)
        t_gu = sb("t_gu", [3 * 2 * RANK, 2, NPAIR, P], F32R)
        t_d = sb("t_d", [3 * 2 * RANK, NPAIR, P], F32R)
        t_masked = sb("t_masked", [P, TG])
        t_rounded = sb("t_rounded", [P, TG], F32R)
        mask_gu = sb("mask_gu", [P, BG // 2])
        mask_d = sb("mask_d", [P, BG])
        gated = sb("gated", [P, 2, TG])
        x1 = sb("x1", [P, 2, TG])
        room = sb("room", [P, KT * TG])
        x_staged = room[:, :].rearrange("p (k n) -> p k n", k=KT)
        x_raw = x_staged[:, 0:2, :]
        q_room = room[:, 2 * TG:KT * TG].rearrange("p (b n) -> p b n", n=QW)
        q_w, q_scale, q_recip, q_value, q_out, q_delta, q_acc, q_acc2 = (q_room[:, i, :] for i in range(8))
        q_mask = sb("q_mask", [P, 6, QW], U8)
        q_a = sb("q_a", [LRANK, P])
        q_b = sb("q_b", [LRANK, QW])
        code = sb("code", [P, NCODE])
        small = sb("small", [P, NCODE])
        amax = sb("amax", [P, 1])
        thr = sb("thr", [P, NCODE + 1])
        idx_raw = sb("idx_raw", [1, BATCH], I32)
        idx_f = sb("idx_f", [1, 2, BATCH])
        idx = sb("idx", [1, BATCH], I32)

        def f32(ap):
            return ap.bitcast(F32)

        FIRST_PARTS = (slice(0, 2), slice(2, 4), slice(4, KT))

        e_all = x1[:, :, :].rearrange("p a n -> p (a n)").rearrange("p (b n) -> p b n", n=KT * H // P)
        e_scale, e_recip, sn, sr, sp_, s1, s2 = (e_all[:, i, :] for i in range(7))
        sx = e_scale

        def bank(name):
            return ctx.enter_context(nc.psum_tensor(name, [P, TG], F32))

        gate_ps = [bank("gate_ps0"), bank("gate_ps1")]
        up_ps = [bank("up_ps0"), bank("up_ps1")]
        t_ps = bank("t_ps")
        out_ps = [bank("out_ps0"), bank("out_ps1")]
        code_ps = bank("code_ps")[:, 0:NCODE]

        idx_loaded, code_loaded, masks_loaded = sem("idx_loaded"), sem("code_loaded"), sem("masks_loaded")
        slog_loaded, scale_stored = sem("slog_loaded"), sem("scale_stored")
        a_gathered, b_gathered, d_gathered = sem("a_gathered"), sem("b_gathered"), sem("d_gathered")
        w_loaded = [sem("w_loaded0"), sem("w_loaded1")]
        x_loaded = [sem("x_loaded0"), sem("x_loaded1")]
        b_loaded, q_loaded, q_ab_loaded = sem("b_loaded"), sem("q_loaded"), sem("q_ab_loaded")
        q_scale_loaded = sem("q_scale_loaded")
        x_first_loaded = [sem(f"x_first_loaded{i}") for i in range(len(FIRST_PARTS))]
        x1_loaded = sem("x1_loaded")
        exp_step = sem("exp_step")
        w_rounded, w_split = sem("w_rounded"), sem("w_split")
        x_rounded, x_split = sem("x_rounded"), sem("x_split")
        b_rounded, b_split = sem("b_rounded"), sem("b_split")
        silu_done, act_rounded = sem("silu_done"), sem("act_rounded")
        prod_done, act_split, evac_done = sem("prod_done"), sem("act_split"), sem("evac_done")
        t_masked_s, t_rounded_s, t_rest_s = sem("t_masked_s"), sem("t_rounded_s"), sem("t_rest_s")
        t_hi_placed, t_lo_placed = sem("t_hi_placed"), sem("t_lo_placed")
        xsum_done = sem("xsum_done")
        x1_stored, x1_free = sem("x1_stored"), sem("x1_free")
        unit_done, x_used, delta_done = sem("unit_done"), sem("x_used"), sem("delta_done")
        q_step, weff_stored, piece_stored = sem("q_step"), sem("weff_stored"), sem("piece_stored")
        setup_step, idx_ready, scale_ready = sem("setup_step"), sem("idx_ready"), sem("scale_ready")

        def loop(engine, end):
            return nc.Fori(0, end, engines=[engine.engine], hint_back_edge=True)

        block = ctx.enter_context(nc.Block())

        @block.sync
        def _(sp):
            def wait(semaphore, value):
                sp.wait_ge(semaphore, value)
                sp.nop(nofuse=True)

            def load_unit(c, half, src):
                if half is not None:
                    wait(w_split, half * 2 + (c - 1))
                sp.dma_start(w_raw[:, c % 2, :], src).then_inc(w_loaded[c % 2], 16)

            def a_gu(g, s):
                return agu_g[bass.ds(g, 1), s, :, :, :, :].rearrange("a p m b n -> (a p) (m b n)")

            def a_d(g, s):
                return ad_g[bass.ds(g, 1), s, :, :, :].rearrange("a p b n -> (a p) (b n)")

            def w_eff(o):
                return weff_d[:, :, o * P:(o + 1) * P]

            def load_x(m, j, src):
                wait(x_split, m - 1)
                sp.dma_start(x_raw[:, j % 2, :], src[:, j, :]).then_inc(x_loaded[j % 2], 16)

            def load_b(n, src, width):
                wait(b_split, n + 1)
                for c in range(3):
                    sp.dma_start(b_raw[32 * c:32 * c + 32, :, 0:width], src).then_inc(b_loaded, 16)

            def adapter(g, b):
                return bass.ds(sp.value_load(idx[0:1, bass.ds(g * BG + b, 1)], min_val=0, max_val=NADAPT - 1), 1)

            def gather_a(g, s, b, one):
                sp.dma_start(agu_g[bass.ds(g, 1), bass.ds(s, 1), :, :, b, :].rearrange("a s p m n -> (a s p) m n"),
                             agu_in[one, :, :, :].rearrange("a p m n -> (a p) m n")).then_inc(a_gathered, 16)

            def gather_b(g, s, b, one):
                rows, pair = slice(b % 2 * RANK, b % 2 * RANK + RANK), bass.ds(s * 2 + b // 2, 1)
                sp.dma_start(bgu_g[bass.ds(g, 1), :, rows, pair, :].rearrange("a t k c n -> (a t) (k c) n"),
                             bgu_in[one, :, :, :].rearrange("a t k n -> (a t) k n")).then_inc(b_gathered, 16)

            def gather_d(g, s, b, one):
                rows, pair = slice(b % 2 * RANK, b % 2 * RANK + RANK), bass.ds(s * 2 + b // 2, 1)
                sp.dma_start(ad_g[bass.ds(g, 1), :, :, bass.ds(s * 4 + b, 1), :].rearrange("a t p b n -> (a t) p (b n)"),
                             ad_in[one, :, :, :].rearrange("a t p n -> (a t) p n")).then_inc(d_gathered, 16)
                sp.dma_start(bd_g[bass.ds(g, 1), :, rows, pair, :].rearrange("a t k c n -> (a t) (k c) n"),
                             bd_in[one, :, :, :].rearrange("a t k n -> (a t) k n")).then_inc(d_gathered, 16)

            sp.dma_start(idx_raw[:, :], idx_in).then_inc(idx_loaded, 16)
            load_unit(U_G0, None, w_in[0, :, :])
            for part, loaded in zip(FIRST_PARTS, x_first_loaded):
                sp.dma_start(x_staged[:, part, :], x_in[0, :, part, :]).then_inc(loaded, 16)
            wait(idx_ready, 1)
            first = [adapter(0, b) for b in range(BG)]
            for s in range(2):
                c = U_A + s
                raw = w_raw[:, c % 2, :].rearrange("p (m b n) -> p m b n", m=2, b=BG // 2)
                for b in range(BG // 2):
                    if s == 1 and b == 0:
                        wait(w_split, c - 1)
                    sp.dma_start(raw[:, :, b, :],
                                 agu_in[first[s * (BG // 2) + b], :, :, :].rearrange("a p m n -> (a p) m n")).then_inc(w_loaded[c % 2], 16)
            for b in range(BG):
                if b == BG // 2:
                    load_unit(U_UP0, 0, w_in[1, :, :])
                gather_b(0, b // 4, b % 4, first[b])

            def b_source(g, n):
                if n < FT:
                    return bgu_g[bass.ds(g, 1), n, :, :, :].rearrange("a r c n -> (a r) c n")
                return bd_g[bass.ds(g, 1), n - FT, :, :, :].rearrange("a r c n -> (a r) c n")

            def ffn(g, last):
                half = g * (U_FFN // 2)

                def before(c):
                    if 5 <= c <= 5 + 2 * NT and c % 2 == 1:
                        q = (c - 5) // 2
                        load_b(g * LN_B + q, b_source(g, q), 2 * P)
                    if 52 <= c <= 73 and (c - 52) % 3 == 0:
                        n = FT + (c - 52) // 3
                        load_b(g * LN_B + n, b_source(g, n), P)
                    if 50 <= c <= 71 and (c - 50) % 3 == 0:
                        j = (c - 50) // 3
                        if last:
                            if j == 0:
                                wait(x1_stored, 16 * HT)
                            load_x((g + 1) * KT + j, j, x1_d[0, :, :, :])
                        else:
                            load_x((g + 1) * KT + j, j, x_in[bass.ds(g + 1, 1), :, :, :].rearrange("a p k n -> (a p) k n"))

                def unit(c):
                    before(c)
                    if U_AD <= c < U_D:
                        load_unit(c, half, a_d(g, c - U_AD))
                    elif c < U_D:
                        load_unit(c, half, w_in[c - U_P, :, :])
                    elif c < U_FFN:
                        load_unit(c, half, w_in[c - U_P - FC, :, :])
                    elif last:
                        load_unit(c, half, w_eff(c - U_FFN))
                    elif c < U_FFN + U_A:
                        load_unit(c, half, w_in[0, :, :])
                    elif c < U_FFN + U_UP0:
                        load_unit(c, half, a_gu(g + 1, c - U_FFN - U_A))
                    else:
                        load_unit(c, half, w_in[1, :, :])

                unit(4)
                wait(b_gathered, (g + 1) * (16 * BG))
                unit(5)
                with loop(sp, 2) as i:
                    for k in range(16):
                        if k % 4 == 0:
                            gather_d(g, i, k // 4, adapter(g, i * 4 + k // 4))
                        if k % 4 == 2 and not last:
                            one = adapter(g + 1, i * 4 + k // 4)
                            gather_a(g + 1, i, k // 4, one)
                            gather_b(g + 1, i, k // 4, one)
                        if k % 2 == 1:
                            q = i * 8 + (k + 1) // 2
                            load_b(g * LN_B + q,
                                   bgu_g[bass.ds(g, 1), bass.ds(q, 1), :, :, :].rearrange("a t r c n -> (a t r) c n"), 2 * P)
                        load_unit(6 + k, half + i * 8,
                                  w_in[bass.ds(i * 16 + (6 + k - U_P), 1), :, :].rearrange("a p n -> (a p) n"))
                wait(d_gathered, (g + 1) * (2 * 16 * BG))
                for c in range(38, U_FFN):
                    unit(c)
                if not last:
                    wait(a_gathered, (g + 1) * (16 * BG))
                for c in range(U_FFN, U_FFN + SLOTS):
                    if last:
                        wait_w_eff(c - U_FFN)
                    unit(c)

            def wait_w_eff(o):
                after = sum(at % H >= (o + 1) * P for at, _ in PIECES[-2:])
                wait(weff_stored, 16 * (NQ - after))

            def second(g, last):
                half = NG * (U_FFN // 2) + g * (HT // 2)
                for c in range(SLOTS, HT if last else HT + SLOTS):
                    if c < HT:
                        wait_w_eff(c)
                    load_unit(c, half, w_eff(c % HT))
                    if c == 5 and not last:
                        wait(x1_stored, (g + 2) * (16 * HT))
                        wait(weff_stored, 16 * NQ)
                        wait(x_split, (g + NG + 1) * KT)
                        sp.dma_start(x_staged, x1_d[bass.ds(g + 1, 1), :, :, :].rearrange("a p k n -> (a p) k n")).then_inc(x1_loaded, 16)

            with loop(sp, NG - 1) as g:
                ffn(g, False)
            ffn(NG - 1, True)
            with loop(sp, NG - 1) as g:
                second(g, False)
            second(NG - 1, True)

        @block.gpsimd
        def _(pool):
            def wait(semaphore, value):
                pool.wait_ge(semaphore, value)
                pool.nop(nofuse=True)

            def load_adapter(g, i):
                at, width = PIECES[i]
                pool.dma_start(q_a[:, :], qa_in[:, bass.ds(g * 8 + at // 256, 1), :].rearrange("r a n -> r (a n)")).then_inc(q_ab_loaded, 16)
                pool.dma_start(q_b[:, 0:width], qb_in[:, at:at + width]).then_inc(q_ab_loaded, 16)

            pool.sem_inc(x1_free, BUFFERS)
            pool.sem_inc(piece_stored, 1)
            load_adapter(0, 0)
            pool.dma_start(code[:, :], code_in[0:1, :].to_broadcast([P, NCODE])).then_inc(code_loaded, 16)
            pool.dma_start(e_scale, slog_in).then_inc(slog_loaded, 16)
            pool.dma_start(mask_gu[:, :], mask_gu_in).then_inc(masks_loaded, 16)
            pool.dma_start(mask_d[:, :], mask_d_in).then_inc(masks_loaded, 16)
            wait(slog_loaded, 16)
            chain = [
                lambda: nc.gpsimd.tensor_scalar(sx, sx, -110.0, 92.0, ALU.max, ALU.min),
                lambda: nc.gpsimd.tensor_scalar(sn, sx, LOG2E, None, ALU.mult),
                lambda: nc.gpsimd.tensor_scalar(sn, sn, ROUND, ROUND, ALU.add, ALU.subtract),
                lambda: nc.gpsimd.tensor_scalar(sr, sn, -LN2_HI, None, ALU.mult),
                lambda: nc.gpsimd.tensor_tensor(sr, sr, sx, ALU.add),
                lambda: nc.gpsimd.tensor_scalar(s1, sn, -LN2_LO, None, ALU.mult),
                lambda: nc.gpsimd.tensor_tensor(sr, sr, s1, ALU.add),
                lambda: nc.gpsimd.tensor_scalar(sp_, sr, EXP_POLY[0], EXP_POLY[1], ALU.mult, ALU.add),
            ]
            for coef in EXP_POLY[2:]:
                chain.append(lambda: nc.gpsimd.tensor_tensor(sp_, sp_, sr, ALU.mult))
                chain.append(lambda c=coef: nc.gpsimd.tensor_scalar(sp_, sp_, c, None, ALU.add))
            chain += [
                lambda: nc.gpsimd.tensor_tensor(sp_, sp_, sr, ALU.mult),
                lambda: nc.gpsimd.tensor_tensor(sp_, sp_, sr, ALU.mult),
                lambda: nc.gpsimd.tensor_tensor(sp_, sp_, sr, ALU.add),
                lambda: nc.gpsimd.tensor_scalar(sp_, sp_, 1.0, None, ALU.add),
                lambda: nc.gpsimd.tensor_scalar(s1, sn, 0.5, None, ALU.mult),
                lambda: nc.gpsimd.tensor_scalar(s1, s1, ROUND, ROUND, ALU.add, ALU.subtract),
                lambda: nc.gpsimd.tensor_tensor(s2, sn, s1, ALU.subtract),
                lambda: nc.gpsimd.tensor_scalar(s1.bitcast(I32), s1, 127.0, 8388608.0, ALU.add, ALU.mult),
                lambda: nc.gpsimd.tensor_scalar(s2.bitcast(I32), s2, 127.0, 8388608.0, ALU.add, ALU.mult),
                lambda: nc.gpsimd.tensor_tensor(sp_, sp_, s1, ALU.mult),
                lambda: nc.gpsimd.tensor_tensor(sx, sp_, s2, ALU.mult),
            ]
            assert len(chain) == EXP_STEPS
            for n, make in enumerate(chain):
                if n:
                    pool.wait_ge(exp_step, n)
                make().then_inc(exp_step, 1)
            wait(scale_ready, 1)
            pool.dma_start(scale_d[0, :, :], e_scale).then_inc(scale_stored, 16)
            pool.dma_start(scale_d[1, :, :], e_recip).then_inc(scale_stored, 16)
            wait(scale_stored, 32)
            scale_row = scale_d.rearrange("a p n -> a (p n)")
            weff_flat = weff_d.rearrange("p k n -> p (k n)")

            def row(g, i, r):
                at, width = PIECES[i]
                return scale_row[r:r + 1, bass.ds(g * QCOLS + at, width)].to_broadcast([P, width])

            def load_piece(g, i):
                at, width = PIECES[i]
                pool.dma_start(q_w[:, 0:width], qw_in[:, bass.ds(g * QCOLS + at, width)]).then_inc(q_loaded, 16)
                pool.dma_start(q_recip[:, 0:width], row(g, i, 1)).then_inc(q_loaded, 16)

            def load_scale(g, i):
                pool.dma_start(q_scale[:, 0:PIECES[i][1]], row(g, i, 0)).then_inc(q_scale_loaded, 16)

            def store_x1(n, j, dst):
                wait(evac_done, n + 1 + BUFFERS)
                pool.dma_start(dst, x1[:, j % 2, :]).then_inc(x1_stored, 16)
                wait(x1_stored, n * 16 + 16)
                pool.sem_inc(x1_free, 1)

            def fetch_after(g, last, i):
                n = g * NPIECE + i
                if i + 1 < NPIECE or not last:
                    after = (g, i + 1) if i + 1 < NPIECE else (g + 1, 0)
                    wait(delta_done, n + 1)
                    load_adapter(*after)
                    wait(q_step, n * QSTEPS + (3 + QSTEPS))
                    load_piece(*after)

            def finish(g, last, i):
                n, (at, width) = g * NPIECE + i, PIECES[i]
                wait(q_step, n * QSTEPS + 2 * QSTEPS)
                if i + 1 < NPIECE:
                    load_scale(g, i + 1)
                elif not last:
                    load_scale(g + 1, 0)
                pool.dma_start(weff_flat[:, bass.ds(g * QCOLS + at, width)], q_out[:, 0:width]).then_inc(weff_stored, 16)
                wait(weff_stored, n * 16 + 16)
                pool.sem_inc(piece_stored, 1)

            def ffn(g, last):
                for i in range(5):
                    fetch_after(g, last, i)
                    finish(g, last, i)
                for i in range(5, NPIECE):
                    fetch_after(g, last, i)
                    for j in range((i - 5) * 4, (i - 5) * 4 + 4):
                        store_x1(g * HT + j, j, x1_d[bass.ds(g, 1), :, j, :].rearrange("a p n -> (a p) n"))
                    finish(g, last, i)

            def second(g):
                for o in range(HT):
                    store_x1(NG * HT + g * HT + o, o, out[bass.ds(g, 1), o, :, :].rearrange("a p n -> (a p) n"))

            wait(x_split, KT)
            load_piece(0, 0)
            load_scale(0, 0)
            with loop(pool, NG - 1) as g:
                ffn(g, False)
            ffn(NG - 1, True)
            with loop(pool, NG) as g:
                second(g)
            wait(x1_stored, 16 * 2 * NG * HT)

        @block.scalar
        def _(act):
            def copy(dst, src):
                return nc.scalar.activation(dst, src, ACT.Copy)

            def round_unit(c, half):
                act.wait_ge(w_loaded[c % 2], 16 * (half + (c // 2 + 1 + MORE_LOADS)))
                copy(w_hi[:, c % SLOTS, :], w_raw[:, c % 2, :]).then_inc(w_rounded, 1)

            def round_x1(g, j):
                act.wait_ge(evac_done, (NG * HT + g * HT) + (j + 1 + BUFFERS))
                copy(x_hi[:, j, :], x_staged[:, j, :]).then_inc(x_rounded, 1)

            def round_b(n, width):
                act.wait_ge(b_loaded, n * 48 + 48)
                copy(b_stack[:, :, 0:width], b_raw[:, :, 0:width]).then_inc(b_rounded, 1)

            def place_t(n, both_sets, dst):
                act.wait_ge(t_masked_s, n + 1)
                copy(t_rounded[:, :], t_masked[:, :]).then_inc(t_rounded_s, 1)
                act.wait_ge(t_rounded_s, n + 1)
                parts = [(c, m, p) for c in range(2) for m in range(2) for p in range(2)]
                for c, m, p in parts:
                    rows = slice(32 * (2 * m + p), 32 * (2 * m + p) + 32)
                    last = copy(dst(slice(32 * c, 32 * c + 32), m, p), f32(t_source(rows, both_sets, m, p)))
                last.then_inc(t_hi_placed, 1)

            def t_source(rows, both_sets, m, p):
                if both_sets:
                    return t_rounded[rows, :].rearrange("r (s p n) -> r s p n", s=2, p=2)[:, :, p, :]
                return t_rounded[rows, (2 * m + p) * P:(2 * m + p + 1) * P]

            def gu_dst(rows, m, p):
                return t_gu[rows, m, :, :].rearrange("r (s p) n -> r s p n", s=2)[:, :, p, :]

            def d_dst(rows, m, p):
                return t_d[rows, 2 * m + p, :]

            def silu_pair(q, k):
                act.wait_ge(act_split, q + 1)
                nc.scalar.activation(gated[:, k % 2, :], gate_ps[k % 2][:, :], ACT.Silu).then_inc(silu_done, 1)

            def round_act(q, k, dst):
                act.wait_ge(prod_done, q + 1 + BUFFERS)
                copy(dst, gated[:, k % 2:k % 2 + 1, :]).then_inc(act_rounded, 1)

            act.wait_ge(w_loaded[0], 16)
            copy(w_hi[:, U_G0, :], w_raw[:, U_G0, :]).then_inc(w_rounded, 1)
            for part, loaded in zip(FIRST_PARTS, x_first_loaded):
                act.wait_ge(loaded, 16)
                for j in range(part.start, part.stop):
                    copy(x_hi[:, j, :], x_staged[:, j, :]).then_inc(x_rounded, 1)
            for c in range(1, SLOTS):
                round_unit(c, 0)

            def ffn(g):
                base, half = g * U_FFN, g * (U_FFN // 2)

                def done(v):
                    act.wait_ge(unit_done, base + (v + 1))

                done(0)
                round_unit(4, half)
                round_b(g * LN_B, 2 * P)
                done(2)
                place_t(2 * g, True, gu_dst)
                round_unit(5, half)
                round_unit(6, half)
                done(3)
                silu_pair(g * FT, 0)
                round_b(g * LN_B + 1, 2 * P)
                round_act(g * FT, 0, act_hi[:, 0:1, :])
                round_unit(7, half)
                with loop(act, 5) as i:
                    for k in range(8):
                        act.wait_ge(unit_done, base + i * 8 + (5 + k))
                        if k % 2 == 1:
                            q = i * 4 + (1 + k // 2)
                            silu_pair(g * FT + q, 1 + k // 2)
                            round_b(g * LN_B + q + 1, 2 * P)
                            round_act(g * FT + q, 1 + k // 2, act_hi[:, bass.ds(q, 1), :])
                        round_unit(8 + k, half + i * 4)
                done(44)
                act.wait_ge(act_split, g * FT + NT + 1)
                nc.scalar.activation(gated[FREST:P, 1, :], gate_ps[1][0:FREST, :], ACT.Silu).then_inc(silu_done, 1)
                act.wait_ge(prod_done, g * FT + FT + BUFFERS)
                copy(act_hi[0:FREST, NT, :], gated[0:FREST, 1, :]).then_inc(act_rounded, 1)
                round_unit(48, half)
                for v in (45, 46):
                    done(v)
                    round_unit(v + 4, half)
                done(47)
                place_t(2 * g + 1, False, d_dst)
                round_unit(51, half)
                with loop(act, 2) as it:
                    for k in range(12):
                        act.wait_ge(unit_done, base + it * 12 + (U_D + 1 + k))
                        if k % 3 == 0:
                            round_b(g * LN_B + it * 4 + (FT + k // 3), P)
                        if k % 3 == 2:
                            j = it * 4 + k // 3
                            act.wait_ge(x_loaded[(k // 3) % 2], 16 * (g * 4 + it * 2 + (k // 3 // 2 + 1)))
                            act.wait_ge(evac_done, g * HT + j + (1 + BUFFERS))
                            copy(x_hi[:, bass.ds(j, 1), :], x_raw[:, (k // 3) % 2:(k // 3) % 2 + 1, :]).then_inc(x_rounded, 1)
                        round_unit(52 + k, half + it * 6)

            def second(g, last):
                base, half = NG * U_FFN + g * HT, NG * (U_FFN // 2) + g * (HT // 2)
                for v in range(HT):
                    if v == HT - 1 and not last:
                        act.wait_ge(x1_loaded, g * 16 + 16)
                        for k in range(KT - 1):
                            act.wait_ge(x_used, g * (KT - 1) + (k + 1))
                            round_x1(g, k)
                    act.wait_ge(unit_done, base + (v + 1))
                    if v == HT - 1 and not last:
                        round_x1(g, v)
                    if v < HT - SLOTS or not last:
                        round_unit(SLOTS + v, half)

            with loop(act, NG) as g:
                ffn(g)
            with loop(act, NG - 1) as g:
                second(g, False)
            second(NG - 1, True)

        @block.vector
        def _(dve):
            def step(n, ins):
                ins.then_inc(setup_step, 1)
                dve.wait_ge(setup_step, n)

            for credited in (prod_done, act_split, evac_done):
                dve.sem_inc(credited, BUFFERS)
            dve.sem_inc(b_split, 1)
            dve.sem_inc(q_step, QSTEPS)

            dve.wait_ge(idx_loaded, 16)
            fa, fb = idx_f[:, 0, :], idx_f[:, 1, :]
            step(1, nc.vector.tensor_copy(fa, idx_raw[:, :]))
            step(2, nc.vector.tensor_scalar(fb, fa, 0.0, float(NADAPT), ALU.is_lt, ALU.mult))
            step(3, nc.vector.tensor_tensor(fa, fa, fb, ALU.add))
            step(4, nc.vector.tensor_scalar(fb, fa, 0.0, float(NADAPT - 1), ALU.max, ALU.min))
            nc.vector.tensor_copy(idx[:, :], fb).then_inc(idx_ready, 1)

            def split_unit(c, u):
                dve.wait_ge(w_rounded, u + 1)
                nc.vector.tensor_tensor(w_lo[:, c % SLOTS, :], w_raw[:, c % 2, :], f32(w_hi[:, c % SLOTS, :]),
                                        ALU.subtract).then_inc(w_split, 1)

            def split_x(m, j, at, staged=False):
                dve.wait_ge(x_rounded, m + 1)
                src = x_staged[:, j:j + 1, :] if staged else x_raw[:, j % 2:j % 2 + 1, :]
                nc.vector.tensor_tensor(x_lo[:, at, :], src, f32(x_hi[:, at, :]),
                                        ALU.subtract).then_inc(x_split, 1)

            def split_b(n, width):
                rows = slice(2 * RANK, 4 * RANK)
                dve.wait_ge(b_rounded, n + 1)
                nc.vector.tensor_tensor(b_stack[rows, :, 0:width], b_raw[rows, :, 0:width],
                                        f32(b_stack[rows, :, 0:width]), ALU.subtract).then_inc(b_split, 1)

            split_unit(0, 0)
            for j in range(KT):
                split_x(j, j, slice(j, j + 1), staged=True)
            split_unit(1, 1)

            dve.wait_ge(code_loaded, 16)
            chain = [
                lambda: nc.vector.tensor_scalar(small[:, :], code[:, :], -1.0, None, ALU.mult),
                lambda: nc.vector.tensor_tensor(small[:, :], small[:, :], code[:, :], ALU.max),
                lambda: nc.vector.reduce_max(amax[:, :], small[:, :], AX.X),
                lambda: nc.vector.tensor_scalar(amax[:, :], amax[:, :], 1e-8, None, ALU.max),
                lambda: nc.vector.reciprocal(amax[:, :], amax[:, :]),
                lambda: nc.vector.tensor_scalar(code[:, :], code[:, :], amax[:, 0:1], None, ALU.mult),
                lambda: nc.vector.tensor_tensor(small[:, 0:NCODE - 1], code[:, 0:NCODE - 1], code[:, 1:NCODE], ALU.add),
                lambda: nc.vector.memset(thr[:, 0:1], -3.4028235e38),
                lambda: nc.vector.memset(thr[:, NCODE:NCODE + 1], 3.4028235e38),
                lambda: nc.vector.tensor_scalar(thr[:, 1:NCODE], small[:, 0:NCODE - 1], 0.5, None, ALU.mult),
            ]
            s = NCODE // 2
            while s:
                mine, below, above = (thr[:, s:NCODE:2 * s], thr[:, 0:NCODE - s:2 * s], thr[:, 2 * s:NCODE + 1:2 * s])
                chain.append(lambda a=mine, b=below: nc.vector.tensor_tensor(a, a, b, ALU.max))
                chain.append(lambda a=mine, b=above: nc.vector.tensor_tensor(a, a, b, ALU.min))
                s //= 2
            chain.append(lambda: nc.vector.tensor_copy(code_ps, code[:, :]))
            for n, make in enumerate(chain):
                step(4 + n + 1, make())

            for c in range(2, SLOTS):
                split_unit(c, c)

            dve.wait_ge(exp_step, EXP_STEPS)
            nc.vector.reciprocal(e_recip, e_scale).then_inc(scale_ready, 1)

            def piece_steps(n, width):
                delta, w, acc = q_delta[:, 0:width], q_value[:, 0:width], q_acc[:, 0:width]
                steps = []

                def add(make, after=None, before=None):
                    at = len(steps)
                    need = at if after is None else after

                    def run():
                        if before:
                            before()
                        if need > 0 or at == 0:
                            dve.wait_ge(q_step, n * QSTEPS + (need + QSTEPS))
                        make().then_inc(q_step, 1)
                    steps.append(run)

                def inputs():
                    dve.wait_ge(q_loaded, n * 32 + 32)
                    dve.wait_ge(delta_done, n + 1)

                add(lambda: nc.vector.tensor_scalar(delta, t_ps[:, 0:width], HALF, None, ALU.mult), before=inputs)
                add(lambda: nc.vector.tensor_tensor(w, q_w[:, 0:width], delta, ALU.add))
                add(lambda: nc.vector.tensor_tensor(w, w, q_recip[:, 0:width], ALU.mult))
                add(lambda: nc.vector.tensor_copy(q_acc2[:, 0:width], code[:, MID:MID + 1].to_broadcast([P, width])),
                    after=0)
                add(lambda: nc.vector.tensor_copy(acc, code[:, 0:1].to_broadcast([P, width])), after=0)

                chains = ((acc, 0), (q_acc2[:, 0:width], MID))

                def above(chain, i, after):
                    first = chains[chain][1]
                    add(lambda: nc.vector.tensor_scalar(q_mask[:, 2 * (i % 3) + chain, 0:width], w,
                                                        thr[:, first + i + 1:first + i + 2], None, ALU.is_gt), after=after)

                def take(chain, i, before=None):
                    target, first = chains[chain]
                    code_of = code_ps[:, first + i + 1:first + i + 2]
                    add(lambda: nc.vector.copy_predicated(target, q_mask[:, 2 * (i % 3) + chain, 0:width],
                                                          code_of.to_broadcast([P, width])), after=0, before=before)

                def settle():
                    at = len(steps)

                    def run():
                        dve.wait_ge(q_step, n * QSTEPS + (at + QSTEPS))
                        dve.nop(nofuse=True)
                    return run

                above(0, 0, len(steps))
                above(1, 0, 0)
                for i in range(MID - 1):
                    if i + 1 < MID - 1:
                        above(0, i + 1, 0)
                        above(1, i + 1, len(steps) - 1)
                        take(0, i)
                    else:
                        take(0, i, settle())
                    take(1, i)
                add(lambda: nc.vector.tensor_scalar(q_mask[:, 2 * ((MID - 1) % 3), 0:width], w,
                                                    thr[:, MID:MID + 1], None, ALU.is_gt))
                add(lambda: nc.vector.copy_predicated(acc, q_mask[:, 2 * ((MID - 1) % 3), 0:width],
                                                      q_acc2[:, 0:width]), after=0, before=settle())
                add(lambda: nc.vector.tensor_tensor(acc, acc, w, ALU.subtract))
                add(lambda: nc.vector.tensor_tensor(acc, acc, w, ALU.add))
                add(lambda: nc.vector.tensor_tensor(acc, acc, q_scale[:, 0:width], ALU.mult),
                    before=lambda: dve.wait_ge(q_scale_loaded, n * 16 + 16))
                add(lambda: nc.vector.tensor_tensor(q_out[:, 0:width], acc, delta, ALU.add),
                    before=lambda: dve.wait_ge(piece_stored, n + 1))
                assert len(steps) == QSTEPS
                return steps

            def share(steps, k, of):
                for run in steps[QSTEPS * k // of:QSTEPS * (k + 1) // of]:
                    run()

            def place_t(n, mask, src, dst, sets):
                shape = dict(a=sets, n=SEQ)
                nc.vector.tensor_tensor(t_masked[:, :].rearrange("p (a m n) -> p a m n", **shape),
                                        t_ps[:, :].rearrange("p (a m n) -> p a m n", **shape),
                                        mask.to_broadcast([P, sets, BG // sets, SEQ]),
                                        ALU.mult).then_inc(t_masked_s, 1)
                dve.wait_ge(t_rounded_s, n + 1)
                nc.vector.tensor_tensor(t_masked[:, :], t_masked[:, :], f32(t_rounded[:, :]),
                                        ALU.subtract).then_inc(t_rest_s, 1)
                dve.wait_ge(t_rest_s, n + 1)
                for m in range(2):
                    for p in range(2):
                        rows = slice(32 * (2 * m + p), 32 * (2 * m + p) + 32)
                        last = nc.vector.tensor_copy(dst(m, p), src(rows, m, p))
                last.then_inc(t_lo_placed, 1)

            LO = slice(4 * RANK, 6 * RANK)

            def place_gu(g):
                place_t(2 * g, mask_gu[:, :].rearrange("p (a m n) -> p a m n", a=1, n=1),
                        lambda rows, m, p: t_masked[rows, :].rearrange("r (s p n) -> r s p n", s=2, p=2)[:, :, p, :],
                        lambda m, p: t_gu[LO, m, :, :].rearrange("r (s p) n -> r s p n", s=2)[:, :, p, :], 2)

            def place_d(g):
                place_t(2 * g + 1, mask_d[:, :].rearrange("p (a m n) -> p a m n", a=1, n=1),
                        lambda rows, m, p: t_masked[rows, (2 * m + p) * P:(2 * m + p + 1) * P],
                        lambda m, p: t_d[LO, 2 * m + p, :], 1)

            def product(q, k):
                dve.wait_ge(silu_done, q + 1)
                nc.vector.tensor_tensor(gated[:, k % 2, :], gated[:, k % 2, :], up_ps[k % 2][:, :],
                                        ALU.mult).then_inc(prod_done, 1)

            def split_act(q, k, at):
                dve.wait_ge(act_rounded, q + 1)
                nc.vector.tensor_tensor(act_lo[:, at, :], gated[:, k % 2:k % 2 + 1, :], f32(act_hi[:, at, :]),
                                        ALU.subtract).then_inc(act_split, 1)

            def residual(n, j, at):
                dve.wait_ge(x1_free, n + 1)
                nc.vector.tensor_tensor(x1[:, j % 2:j % 2 + 1, :], f32(x_hi[:, at, :]), f32(x_lo[:, at, :]),
                                        ALU.add).then_inc(xsum_done, 1)

            def evacuate(n, j):
                dve.wait_ge(xsum_done, n + 1)
                nc.vector.tensor_tensor(x1[:, j % 2, :], x1[:, j % 2, :], out_ps[j % 2][:, :],
                                        ALU.add).then_inc(evac_done, 1)

            dve.wait_ge(masks_loaded, 32)

            def ffn(g):
                base = g * U_FFN

                def done(v):
                    dve.wait_ge(unit_done, base + (v + 1))

                done(0)
                split_unit(4, base + 4)
                split_b(g * LN_B, 2 * P)
                done(2)
                place_gu(g)
                split_unit(5, base + 5)
                split_unit(6, base + 6)
                done(3)
                product(g * FT, 0)
                split_b(g * LN_B + 1, 2 * P)
                split_act(g * FT, 0, slice(0, 1))
                split_unit(7, base + 7)
                with loop(dve, 5) as i:
                    steps = piece_steps(g * NPIECE + i, 256)
                    for k in range(8):
                        dve.wait_ge(unit_done, base + i * 8 + (5 + k))
                        if k % 2 == 1:
                            q = i * 4 + (1 + k // 2)
                            product(g * FT + q, 1 + k // 2)
                            split_b(g * LN_B + q + 1, 2 * P)
                            split_act(g * FT + q, 1 + k // 2, bass.ds(q, 1))
                        split_unit(8 + k, base + i * 8 + (8 + k))
                        share(steps, k, 8)
                done(44)
                dve.wait_ge(silu_done, g * FT + 22)
                nc.vector.tensor_tensor(gated[0:FREST, 1, :], gated[FREST:P, 1, :], gate_ps[1][FREST:P, :],
                                        ALU.mult).then_inc(prod_done, 1)
                dve.wait_ge(act_rounded, g * FT + 22)
                nc.vector.tensor_tensor(act_lo[0:FREST, NT, :], gated[0:FREST, 1, :],
                                        f32(act_hi[0:FREST, NT, :]), ALU.subtract).then_inc(act_split, 1)
                split_unit(48, base + 48)
                for v in (45, 46):
                    done(v)
                    split_unit(v + 4, base + v + 4)
                done(47)
                place_d(g)
                split_unit(51, base + 51)
                with loop(dve, 2) as it:
                    steps = piece_steps(g * NPIECE + it + 5, PIECES[5][1])
                    for k in range(12):
                        j = it * 4 + k // 3
                        if k % 3 == 2:
                            residual(g * HT + j, k // 3, bass.ds(j, 1))
                        dve.wait_ge(unit_done, base + it * 12 + (U_D + 1 + k))
                        if k % 3 == 0:
                            split_b(g * LN_B + FT + j, P)
                        if k % 3 == 2:
                            evacuate(g * HT + j, k // 3)
                            split_x((g + 1) * KT + j, k // 3, bass.ds(j, 1))
                        split_unit(52 + k, base + it * 12 + (52 + k))
                        share(steps, k, 12)

            def second(g, last):
                base = NG * U_FFN + g * HT
                m = (NG + 1) * KT + g * KT
                for v in range(HT):
                    n = NG * HT + g * HT + v
                    if v == HT - 1 and not last:
                        for k in range(KT - 1):
                            split_x(m + k, k, slice(k, k + 1), staged=True)
                    residual(n, v, slice(v, v + 1))
                    dve.wait_ge(unit_done, base + (v + 1))
                    evacuate(n, v)
                    if v == HT - 1 and not last:
                        split_x(m + v, v, slice(v, v + 1), staged=True)
                    if v < HT - SLOTS or not last:
                        split_unit(SLOTS + v, base + SLOTS + v)

            with loop(dve, NG) as g:
                ffn(g)
            with loop(dve, NG - 1) as g:
                second(g, False)
            second(NG - 1, True)

        @block.tensor
        def _(pe):
            mm = nc.tensor.matmul

            def three(out_ap, w_hi_ap, w_lo_ap, m_hi, m_lo, start, stop=False):
                mm(out_ap, w_hi_ap, m_hi, start=start, stop=False)
                mm(out_ap, w_hi_ap, m_lo, start=False, stop=False)
                return mm(out_ap, w_lo_ap, m_hi, start=False, stop=stop)

            def unit(slot, out_ap, moving, start=True, stop=False, tiles=KT, wait=None, mark=None):
                for k in range(tiles):
                    if wait:
                        wait(k)
                    m_hi, m_lo = moving(k)
                    n = m_hi.shape[0]
                    cols = slice(k * P, (k + 1) * P)
                    last = three(out_ap, w_hi[0:n, slot, cols], w_lo[0:n, slot, cols], m_hi, m_lo,
                                 start and k == 0, stop and k == tiles - 1)
                    if mark:
                        mark(k, last)
                return last

            def x_moving(k):
                return x_hi[:, k, :], x_lo[:, k, :]

            def lora(out_tile, b_ap, t_ap, stop=True):
                for pair in range(NPAIR):
                    last = mm(out_tile[:, pair * P:(pair + 1) * P], b_ap[:, pair, :], t_ap[:, pair, :],
                              start=False, stop=stop and pair == NPAIR - 1)
                return last

            def delta(n, width, read):
                pe.wait_ge(t_masked_s, read)
                pe.wait_ge(q_ab_loaded, n * 32 + 32)
                pe.wait_ge(q_step, n * QSTEPS + 1)
                mm(t_ps[:, 0:width], q_a[:, :], q_b[:, 0:width], start=True, stop=True).then_inc(delta_done, 1)

            def pair(base, c, q, k, n_b):
                pe.wait_ge(w_split, base + c + 1)
                pe.wait_ge(prod_done, q + 1)
                unit(c % SLOTS, gate_ps[k % 2][:, :], x_moving)
                pe.wait_ge(b_split, n_b + 2)
                lora(gate_ps[k % 2], b_stack[:, :, 0:P], t_gu[:, 0, :, :]).then_inc(unit_done, 1)

            def pair_up(base, c, k):
                pe.wait_ge(w_split, base + c + 1)
                unit(c % SLOTS, up_ps[k % 2][:, :], x_moving)
                lora(up_ps[k % 2], b_stack[:, :, P:2 * P], t_gu[:, 1, :, :]).then_inc(unit_done, 1)

            def ffn(g):
                base = g * U_FFN
                pe.wait_ge(w_split, base + U_G0 + 1)
                pe.wait_ge(prod_done, g * FT + 1)
                unit(U_G0 % SLOTS, gate_ps[0][:, :], x_moving,
                     wait=lambda k: pe.wait_ge(x_split, g * KT + (k + 1))).then_inc(unit_done, 1)
                for s in range(2):
                    pe.wait_ge(w_split, base + (U_A + s + 1))
                    cols = slice(s * TG // 2, (s + 1) * TG // 2)
                    for k in range(KT):
                        last = three(t_ps[:, cols], w_hi[:, U_A + s, k::KT], w_lo[:, U_A + s, k::KT],
                                     x_hi[:, k, cols], x_lo[:, k, cols], k == 0, k == KT - 1)
                    last.then_inc(unit_done, 1)
                pe.wait_ge(w_split, base + U_UP0 + 1)
                unit(U_UP0 % SLOTS, up_ps[0][:, :], x_moving)
                pe.wait_ge(b_split, g * LN_B + 2)
                pe.wait_ge(t_hi_placed, 2 * g + 1)
                pe.wait_ge(t_lo_placed, 2 * g + 1)
                lora(gate_ps[0], b_stack[:, :, 0:P], t_gu[:, 0, :, :])
                lora(up_ps[0], b_stack[:, :, P:2 * P], t_gu[:, 1, :, :]).then_inc(unit_done, 1)
                with loop(pe, 5) as i:
                    for k in range(8):
                        if k == 1:
                            delta(g * NPIECE + i, 256, 2 * g + 1)
                        q = i * 4 + (1 + k // 2)
                        if k % 2 == 0:
                            pair(base + i * 8, 4 + k, g * FT + q, 1 + k // 2, g * LN_B + q)
                        else:
                            pair_up(base + i * 8, 4 + k, 1 + k // 2)
                pe.wait_ge(w_split, base + U_M + 1)
                pe.wait_ge(prod_done, g * FT + NT + 1)
                unit(U_M % SLOTS, gate_ps[1][:, :], x_moving)
                pe.wait_ge(b_split, g * LN_B + FT + 1)
                lora(gate_ps[1], b_stack[:, :, 0:P], t_gu[:, 0, :, :], stop=False)
                lora(gate_ps[1], b_stack[:, :, P:2 * P], t_gu[:, 1, :, :]).then_inc(unit_done, 1)

                def act_moving(t):
                    rows = FREST if t == NT else P
                    return act_hi[0:rows, t, :], act_lo[0:rows, t, :]

                for s in range(FC):
                    c = U_AD + s
                    pe.wait_ge(w_split, base + c + 1)
                    for k in range(min(KT, FT - s * KT)):
                        t = s * KT + k
                        m_hi, m_lo = act_moving(t)
                        n = m_hi.shape[0]
                        pe.wait_ge(act_split, g * FT + (t + 1 + BUFFERS))
                        last = three(t_ps[:, :], w_hi[0:n, c % SLOTS, k::KT], w_lo[0:n, c % SLOTS, k::KT], m_hi, m_lo,
                                     t == 0, t == FT - 1)
                    last.then_inc(unit_done, 1)
                with loop(pe, 2) as it:
                    for k in range(12):
                        c = U_D + k
                        jj = k // 3
                        s = k % 3
                        n = g * HT + it * 4 + jj
                        pe.wait_ge(w_split, base + it * 12 + (c + 1))
                        if s == 0:
                            pe.wait_ge(evac_done, n + 1)
                        last = unit(c % SLOTS, out_ps[jj % 2][:, :], lambda k: act_moving(s * KT + k), start=s == 0,
                                    tiles=min(KT, FT - s * KT))
                        if s == 2:
                            if k == 2:
                                pe.wait_ge(t_hi_placed, 2 * g + 2)
                                pe.wait_ge(t_lo_placed, 2 * g + 2)
                            pe.wait_ge(b_split, g * LN_B + it * 4 + (FT + jj + 2))
                            last = lora(out_ps[jj % 2], b_stack[:, :, 0:P], t_d[:, :, :])
                        last.then_inc(unit_done, 1)
                        if k == 1:
                            delta(g * NPIECE + it + 5, PIECES[5][1], 2 * g + 2)

            def second(g):
                base = NG * U_FFN + g * HT
                for o in range(HT):
                    pe.wait_ge(w_split, base + o + 1)
                    pe.wait_ge(evac_done, g * HT + (NG * HT + o + 1))

                    def wait(k):
                        pe.wait_ge(x_split, NG * KT + g * KT + (k + 1))

                    def mark(k, last):
                        if k < KT - 1:
                            last.then_inc(x_used, 1)

                    unit(o % SLOTS, out_ps[o % 2][:, :], x_moving, stop=True, wait=wait if o == 0 else None,
                         mark=mark if o == HT - 1 else None).then_inc(unit_done, 1)

            with loop(pe, NG) as g:
                ffn(g)
            with loop(pe, NG) as g:
                second(g)


def kernel(**inputs):
    import numpy as np
    import concourse.bacc as bacc
    from concourse.bass_utils import run_bass_kernel_spmd

    def tiles(w, n_k, n_m):
        return w.reshape(n_m, -1, n_k, P).transpose(0, 3, 2, 1)

    def padded(a, axis, size):
        shape = list(a.shape)
        shape[axis] = size - shape[axis]
        return np.concatenate([a, np.zeros(shape, a.dtype)], axis)

    x = np.asarray(inputs["x"])
    w_gate, w_up, w_down = (np.asarray(inputs[f"L0_cond_W_{n}"]) for n in ("gate", "up", "down"))
    a_gate, a_up, a_down = (np.asarray(inputs[f"L0_cond_A_{n}"])[0] for n in ("gate", "up", "down"))
    b_gate, b_up, b_down = (np.asarray(inputs[f"L0_cond_B_{n}"])[0] for n in ("gate", "up", "down"))
    whole = NT * P
    FP = FC * KT * P

    gate, up = tiles(w_gate[:whole], KT, NT), tiles(w_up[:whole], KT, NT)
    rest = tiles(np.concatenate([w_gate[whole:], w_up[whole:]]), KT, 1)
    down = padded(w_down, 1, FP).reshape(HT, P, FC, KT, P).transpose(0, 2, 4, 3, 1)
    units = np.concatenate([np.stack([gate, up], 1).reshape(2 * NT, P, UNIT), rest.reshape(1, P, UNIT),
                            down.reshape(HT * FC, P, UNIT)])
    agu = np.stack([a_gate, a_up], 1).reshape(NADAPT, 2, RANK, KT, P).transpose(0, 4, 1, 2, 3)
    bt_gate, bt_up = b_gate.transpose(0, 2, 1), b_up.transpose(0, 2, 1)
    zero = np.zeros((NADAPT, RANK, FREST), b_gate.dtype)
    side = [np.concatenate([bt_gate[:, :, :whole], bt_gate[:, :, whole:], zero], 2),
            np.concatenate([bt_up[:, :, :whole], zero, bt_up[:, :, whole:]], 2)]
    bgu = np.stack(side, 2).reshape(NADAPT, RANK, 2, FT, P).transpose(0, 3, 1, 2, 4)
    ad = padded(a_down, 2, FP).reshape(NADAPT, RANK, FC, KT, P).transpose(0, 2, 4, 1, 3)
    bd = b_down.transpose(0, 2, 1).reshape(NADAPT, RANK, HT, P).transpose(0, 2, 1, 3)
    lora_a, lora_b = np.asarray(inputs["L1_cond_lora_A"]), np.asarray(inputs["L1_cond_lora_B"])
    qa = np.repeat(lora_a.reshape(LRANK, KT, 1, P), 4, 2)
    qb = np.concatenate([lora_b.T, lora_b.T], 1)

    rows, cols = np.arange(P)[:, None], np.arange(BG)[None, :]
    arrays = {
        "x_in": x.reshape(NG, TG, KT, P).transpose(0, 3, 2, 1),
        "idx_in": np.asarray(inputs["itok_B_2_6"]).reshape(1, BATCH),
        "code_in": np.asarray(inputs["condB_codebook"]).reshape(1, NCODE),
        "w_in": units,
        "agu_in": agu.reshape(NADAPT, P, 2, RANK * KT),
        "bgu_in": bgu.reshape(NADAPT, FT, RANK, 2 * P),
        "ad_in": ad.reshape(NADAPT, FC, P, RANK * KT),
        "bd_in": bd,
        "qw_in": np.asarray(inputs["L1_cond_weight"]).reshape(H, KT, P).transpose(2, 1, 0).reshape(P, KT * H),
        "slog_in": np.asarray(inputs["L1_cond_scale_log"]).reshape(H, KT).T.reshape(P, KT * H // P),
        "qa_in": qa.reshape(LRANK, 4 * KT, P),
        "qb_in": qb,
        "mask_gu_in": np.where(rows % 64 // RANK == cols[:, :BG // 2], 0.5, 0.0).astype(np.float32),
        "mask_d_in": np.where(rows // RANK == cols, 0.5, 0.0).astype(np.float32),
    }
    nc = bacc.Bacc("TRN2", target_bir_lowering=False, num_devices=1)
    arrays = {n: np.ascontiguousarray(a) for n, a in arrays.items()}
    aps = {n: nc.dram_tensor(n, a.shape, mybir.dt.from_np(a.dtype), kind="ExternalInput").ap()
           for n, a in arrays.items()}
    out = nc.dram_tensor("out", [NG, HT, P, TG], F32, kind="ExternalOutput").ap()
    build(nc, **aps, out=out)
    got = run_bass_kernel_spmd(nc, [arrays], core_ids=[0]).results[0]["out"]
    return np.ascontiguousarray(np.asarray(got).transpose(0, 3, 1, 2)).reshape(BATCH, SEQ, H)
```
